# Optimizing a Trainium2 kernel written in Bass

```python
import numpy as np
import jax
import jax.numpy as jnp

def _softmax(x, axis=-1):
    return jax.nn.softmax(x, axis=axis)

def _gelu(x):
    return jax.nn.gelu(x, approximate=True)

def _silu(x):
    return jax.nn.silu(x)

def _sigmoid(x):
    return jax.nn.sigmoid(x)

def _layernorm(x, axis=-1, eps=1e-05):
    m = jnp.mean(x, axis=axis, keepdims=True)
    v = jnp.var(x, axis=axis, keepdims=True)
    return (x - m) / jnp.sqrt(v + eps)

def _scatter_add(tgt, idx, src, axis=0):
    return tgt.at[idx].add(src)

def _segment_sum(src, seg, n):
    return jax.ops.segment_sum(src, seg, n)
kernel_name = 'mk_flamingo_gated_d4_seqx_r4_42fd64'

def setup_inputs(seed: int=0):
    np.random.seed(seed)
    _w = jnp.asarray

    def _rec_inputs():
        import jax
        import jax.numpy as jnp
        _rk = jax.random.key(seed)
        x = -0.0003929 + 0.9999 * jax.random.normal(jax.random.fold_in(_rk, 1), (2, 1024, 256), jnp.float32)
        _lenS = 1024 - jax.random.randint(jax.random.fold_in(_rk, 7), (2,), 0, max(1, 1024 // 4) + 1, jnp.int32)
        _lenS2 = 77 - jax.random.randint(jax.random.fold_in(_rk, 8), (2,), 0, max(1, 77 // 4) + 1, jnp.int32)
        _ctx_768P = jax.random.normal(jax.random.fold_in(_rk, 11), (2, 16, 192), jnp.float32)
        _ctx_768c = jax.random.dirichlet(jax.random.fold_in(_rk, 511), 0.3 * jnp.ones((16,), jnp.float32), (2, 77))
        _ctx_768t = jnp.einsum('bsk,bkd->bsd', _ctx_768c, _ctx_768P)
        _ctx_768t = _ctx_768t * jax.lax.rsqrt(jnp.mean(jnp.square(_ctx_768t)) + 1e-12) * 0.953939
        ctx_768 = -7.36909e-05 + 0.999899 * (_ctx_768t + 0.3 * jax.random.normal(jax.random.fold_in(_rk, 611), (2, 77, 192), jnp.float32))
        _validS = jnp.arange(1024)[None, :] < _lenS[:, None]
        _validS2 = jnp.arange(77)[None, :] < _lenS2[:, None]
        _causal = jnp.tril(jnp.ones((1024, 1024), dtype=bool))
        mask_BxS2_bk0 = jnp.logical_not(jnp.broadcast_to(_validS2[:, :], (2, 77)))
        _g = jax.random.normal(jax.random.fold_in(_rk, 9001), (2, 4), jnp.float32)
        _g = jnp.sign(_g) * jnp.maximum(jnp.abs(_g), 1.0) + (_g == 0) * 1.0
        g_xattn = _g[0]
        g_ffn = _g[1]
        return (x, ctx_768, mask_BxS2_bk0, g_xattn, g_ffn)
    x, ctx_768, mask_BxS2_bk0, g_xattn, g_ffn = _rec_inputs()

    def _L0_xattn_setup():
        import jax, jax.numpy as jnp
        import numpy as np
        EPS = 1e-05

        def layernorm(x, g, b):
            mu = jnp.mean(x, axis=-1, keepdims=True)
            var = jnp.mean(jnp.square(x - mu), axis=-1, keepdims=True)
            return (x - mu) * jax.lax.rsqrt(var + EPS) * g + b
        key = jax.random.key(seed)
        ks = jax.random.split(key, 12)
        B, L1, L2 = (8, 512, 512)
        D1, D2, E = (256, 192, 256)
        s1, s2, se = (D1 ** (-0.5), D2 ** (-0.5), E ** (-0.5))
        return {'modality1': jax.random.normal(ks[0], (B, L1, D1), jnp.float32), 'modality2': jax.random.normal(ks[1], (B, L2, D2), jnp.float32), 'ln1_g': jnp.ones((D1,), jnp.float32), 'ln1_b': jnp.zeros((D1,), jnp.float32), 'ln2_g': jnp.ones((D2,), jnp.float32), 'ln2_b': jnp.zeros((D2,), jnp.float32), 'Wq': jax.random.normal(ks[2], (D1, E), jnp.float32) * s1, 'bq': jax.random.normal(ks[3], (E,), jnp.float32) * 0.01, 'Wk': jax.random.normal(ks[4], (D2, E), jnp.float32) * s2, 'bk': jax.random.normal(ks[5], (E,), jnp.float32) * 0.01, 'Wv': jax.random.normal(ks[6], (D2, E), jnp.float32) * s2, 'bv': jax.random.normal(ks[7], (E,), jnp.float32) * 0.01, 'Wo': jax.random.normal(ks[8], (E, D1), jnp.float32) * se, 'bo': jax.random.normal(ks[9], (D1,), jnp.float32) * 0.01}
    _L0_xattn_all = _L0_xattn_setup()
    _L0_xattn_in = {k: v for k, v in _L0_xattn_all.items() if k in ('ln1_g', 'ln1_b', 'ln2_g', 'ln2_b', 'Wq', 'bq', 'Wk', 'bk', 'Wv', 'bv', 'Wo', 'bo')}
    del _L0_xattn_all

    def _L0_ffn_setup():
        import jax, jax.numpy as jnp
        import numpy as np
        B, S, H, E, K = (2, 256, 256, 8, 2)
        F = 4 * H
        key = jax.random.key(seed)
        ks = jax.random.split(key, 8)
        std = 0.02
        return {'x': jax.random.normal(ks[0], (B, S, H), jnp.float32), 'gate_w': jax.random.normal(ks[1], (E, H), jnp.float32) * (std / np.sqrt(H)), 'gate_bias': jnp.zeros((E,), jnp.float32), 'Wu': jax.random.normal(ks[2], (E, F, H), jnp.float32) * std, 'bu': jnp.zeros((E, F), jnp.float32), 'Wd': jax.random.normal(ks[3], (E, H, F), jnp.float32) * std, 'bd': jnp.zeros((E, H), jnp.float32), 'sWu': jax.random.normal(ks[4], (F, H), jnp.float32) * std, 'sbu': jnp.zeros((F,), jnp.float32), 'sWd': jax.random.normal(ks[5], (H, F), jnp.float32) * std, 'sbd': jnp.zeros((H,), jnp.float32)}
    _L0_ffn_all = _L0_ffn_setup()
    _L0_ffn_in = {k: v for k, v in _L0_ffn_all.items() if k in ('gate_w', 'gate_bias', 'Wu', 'bu', 'Wd', 'bd', 'sWu', 'sbu', 'sWd', 'sbd')}
    del _L0_ffn_all

    def _L1_xattn_setup():
        import jax, jax.numpy as jnp
        import numpy as np
        DIM_IN, DIM_LAT, DIM_HEAD = (192, 256, 64)
        INNER = max(DIM_LAT, DIM_IN)
        HEADS = INNER // DIM_HEAD
        SCALE = DIM_HEAD ** (-0.5)
        RMS_EPS = 1e-08
        LN_EPS = 1e-05

        def layernorm(x, g, b):
            mu = jnp.mean(x, axis=-1, keepdims=True)
            var = jnp.mean((x - mu) ** 2, axis=-1, keepdims=True)
            return (x - mu) * jax.lax.rsqrt(var + LN_EPS) * g + b

        def rmsnorm(x, gamma):
            norm = jnp.sqrt(jnp.sum(x * x, axis=-1, keepdims=True)) * x.shape[-1] ** (-0.5)
            return x / jnp.maximum(norm, RMS_EPS) * gamma
        key = jax.random.key(seed)
        ks = jax.random.split(key, 12)
        b, n, m = (4, 1024, 128)
        x = jax.random.normal(ks[0], (b, n, DIM_IN), jnp.float32)
        latents = jax.random.normal(ks[1], (b, m, DIM_LAT), jnp.float32)
        mask = jax.random.randint(ks[2], (b, n), 0, 2).astype(bool)
        s = lambda k, sh, fan: jax.random.normal(k, sh, jnp.float32) * fan ** (-0.5)
        return {'x': x, 'latents': latents, 'mask': mask, 'ln_x_g': jnp.ones((DIM_IN,), jnp.float32), 'ln_x_b': jnp.zeros((DIM_IN,), jnp.float32), 'ln_l_g': jnp.ones((DIM_LAT,), jnp.float32), 'ln_l_b': jnp.zeros((DIM_LAT,), jnp.float32), 'qn_g': jnp.ones((DIM_HEAD,), jnp.float32), 'kn_g': jnp.ones((DIM_HEAD,), jnp.float32), 'Wq': s(ks[3], (INNER, DIM_LAT), DIM_LAT), 'Wkv': s(ks[4], (2 * INNER, DIM_IN), DIM_IN), 'Wlkv': s(ks[5], (2 * INNER, DIM_LAT), DIM_LAT), 'Wo': s(ks[6], (DIM_LAT, INNER), INNER), 'bo': jnp.zeros((DIM_LAT,), jnp.float32)}
    _L1_xattn_all = _L1_xattn_setup()
    _L1_xattn_in = {k: v for k, v in _L1_xattn_all.items() if k in ('ln_x_g', 'ln_x_b', 'ln_l_g', 'ln_l_b', 'qn_g', 'kn_g', 'Wq', 'Wkv', 'Wlkv', 'Wo', 'bo')}
    del _L1_xattn_all

    def _L1_ffn_setup():
        import jax, jax.numpy as jnp
        import numpy as np
        TOP_K = 2
        key = jax.random.key(seed)
        k1, k2, k3 = jax.random.split(key, 3)
        B, S, H, E = (4, 512, 256, 8)
        x = jax.random.normal(k1, (B, S, H), dtype=jnp.float32)
        gate_w = jax.random.normal(k2, (E, H), dtype=jnp.float32) / np.sqrt(H)
        gate_b = jnp.zeros((E,), dtype=jnp.float32)
        expert_w = jax.random.normal(k3, (E, H, H), dtype=jnp.float32) / np.sqrt(H)
        expert_b = jnp.zeros((E, H), dtype=jnp.float32)
        return {'x': x, 'gate_w': gate_w, 'gate_b': gate_b, 'expert_w': expert_w, 'expert_b': expert_b}
    _L1_ffn_all = _L1_ffn_setup()
    _L1_ffn_in = {k: v for k, v in _L1_ffn_all.items() if k in ('gate_w', 'gate_b', 'expert_w', 'expert_b')}
    del _L1_ffn_all

    def _L2_xattn_setup():
        import jax, jax.numpy as jnp
        import numpy as np
        QUERY_DIM, KV_DIM, EMBED_DIM, NUM_HEADS = (256, 192, 256, 16)
        HEAD_DIM = EMBED_DIM // NUM_HEADS
        SCALE = HEAD_DIM ** (-0.5)
        LN_EPS = 1e-05

        def _l2norm(x, eps=1e-12):
            n = jnp.sqrt(jnp.sum(x * x, axis=-1, keepdims=True))
            return x / jnp.maximum(n, eps)
        key = jax.random.key(seed)
        ks = jax.random.split(key, 12)
        B, Nq, Nk = (2, 512, 512)
        s = lambda d: 1.0 / np.sqrt(d)
        return {'query': jax.random.normal(ks[0], (B, Nq, QUERY_DIM), jnp.float32), 'key': jax.random.normal(ks[1], (B, Nk, KV_DIM), jnp.float32), 'value': jax.random.normal(ks[2], (B, Nk, KV_DIM), jnp.float32), 'Wq': jax.random.normal(ks[3], (QUERY_DIM, EMBED_DIM), jnp.float32) * s(QUERY_DIM), 'bq': jnp.zeros((EMBED_DIM,), jnp.float32), 'Wk': jax.random.normal(ks[4], (KV_DIM, EMBED_DIM), jnp.float32) * s(KV_DIM), 'bk': jnp.zeros((EMBED_DIM,), jnp.float32), 'Wv': jax.random.normal(ks[5], (KV_DIM, EMBED_DIM), jnp.float32) * s(KV_DIM), 'bv': jnp.zeros((EMBED_DIM,), jnp.float32), 'Wo': jax.random.normal(ks[6], (EMBED_DIM, EMBED_DIM), jnp.float32) * s(EMBED_DIM), 'bo': jnp.zeros((EMBED_DIM,), jnp.float32), 'ln_gamma': jnp.ones((EMBED_DIM,), jnp.float32), 'ln_beta': jnp.zeros((EMBED_DIM,), jnp.float32)}
    _L2_xattn_all = _L2_xattn_setup()
    _L2_xattn_in = {k: v for k, v in _L2_xattn_all.items() if k in ('Wq', 'bq', 'Wk', 'bk', 'Wv', 'bv', 'Wo', 'bo', 'ln_gamma', 'ln_beta')}
    del _L2_xattn_all

    def _L2_ffn_setup():
        import jax, jax.numpy as jnp
        import numpy as np
        B, T, D = (2, 512, 256)
        DCD = 1024
        RET = 128
        NEXP = 1024
        NKEYS = 64
        H = 4
        KPH = 8
        key = jax.random.key(seed)
        ks = jax.random.split(key, 10)
        s = lambda k, shape, scale: jax.random.normal(k, shape, jnp.float32) * scale
        return {'hidden_states': jax.random.normal(ks[0], (B, T, D), jnp.float32), 'Wg': s(ks[1], (D, DCD), 0.02), 'bg': jnp.zeros((DCD,), jnp.float32), 'Wu': s(ks[2], (D, DCD), 0.02), 'bu': jnp.zeros((DCD,), jnp.float32), 'Wd': s(ks[3], (DCD, D), 0.02), 'bd': jnp.zeros((D,), jnp.float32), 'Wq': s(ks[4], (D, RET * H), 0.02), 'keys': s(ks[5], (H, NKEYS, 2, RET // 2), 0.02), 'down_embed': s(ks[6], (NEXP, D), 0.02), 'up_embed': s(ks[7], (NEXP, D), 0.02)}
    _L2_ffn_all = _L2_ffn_setup()
    _L2_ffn_in = {k: v for k, v in _L2_ffn_all.items() if k in ('Wg', 'bg', 'Wu', 'bu', 'Wd', 'bd', 'Wq', 'keys', 'down_embed', 'up_embed')}
    del _L2_ffn_all

    def _L3_xattn_setup():
        import jax, jax.numpy as jnp
        import numpy as np
        HEADS = 8
        DIM_HEAD = 64
        QUERY_DIM = 256
        CONTEXT_DIM = 192
        INNER = HEADS * DIM_HEAD
        key = jax.random.key(seed)
        ks = jax.random.split(key, 7)
        B, Sq, Skv = (4, 1024, 256)
        x = jax.random.normal(ks[0], (B, Sq, QUERY_DIM), dtype=jnp.float32)
        context = jax.random.normal(ks[1], (B, Skv, CONTEXT_DIM), dtype=jnp.float32)
        Wq = jax.random.normal(ks[2], (QUERY_DIM, INNER), dtype=jnp.float32) * QUERY_DIM ** (-0.5)
        Wk = jax.random.normal(ks[3], (CONTEXT_DIM, INNER), dtype=jnp.float32) * CONTEXT_DIM ** (-0.5)
        Wv = jax.random.normal(ks[4], (CONTEXT_DIM, INNER), dtype=jnp.float32) * CONTEXT_DIM ** (-0.5)
        Wo = jax.random.normal(ks[5], (INNER, QUERY_DIM), dtype=jnp.float32) * INNER ** (-0.5)
        bo = jax.random.normal(ks[6], (QUERY_DIM,), dtype=jnp.float32) * 0.01
        return {'x': x, 'context': context, 'Wq': Wq, 'Wk': Wk, 'Wv': Wv, 'Wo': Wo, 'bo': bo}
    _L3_xattn_all = _L3_xattn_setup()
    _L3_xattn_in = {k: v for k, v in _L3_xattn_all.items() if k in ('Wq', 'Wk', 'Wv', 'Wo', 'bo')}
    del _L3_xattn_all

    def _L3_ffn_setup():
        import jax, jax.numpy as jnp
        import numpy as np
        from jax import lax
        D = 256
        H = 1024
        E = 8
        TOPK = 2
        key = jax.random.key(seed)
        ks = jax.random.split(key, 7)
        s = 0.02
        return {'x': jax.random.normal(ks[0], (2, 512, D), dtype=jnp.float32), 'W1': jax.random.normal(ks[1], (E, D, H), dtype=jnp.float32) * s, 'b1': jnp.zeros((E, H), dtype=jnp.float32), 'W2': jax.random.normal(ks[2], (E, H, D), dtype=jnp.float32) * s, 'b2': jnp.zeros((E, D), dtype=jnp.float32), 'Wr': jax.random.normal(ks[3], (D, E), dtype=jnp.float32) * s, 'br': jnp.zeros((E,), dtype=jnp.float32)}
    _L3_ffn_all = _L3_ffn_setup()
    _L3_ffn_in = {k: v for k, v in _L3_ffn_all.items() if k in ('W1', 'b1', 'W2', 'b2', 'Wr', 'br')}
    del _L3_ffn_all
    return {'x': x, 'ctx_768': ctx_768, 'mask_BxS2_bk0': mask_BxS2_bk0, 'g_xattn': g_xattn, 'g_ffn': g_ffn, 'L0_xattn_ln1_g': _L0_xattn_in['ln1_g'], 'L0_xattn_ln1_b': _L0_xattn_in['ln1_b'], 'L0_xattn_ln2_g': _L0_xattn_in['ln2_g'], 'L0_xattn_ln2_b': _L0_xattn_in['ln2_b'], 'L0_xattn_Wq': _L0_xattn_in['Wq'], 'L0_xattn_bq': _L0_xattn_in['bq'], 'L0_xattn_Wk': _L0_xattn_in['Wk'], 'L0_xattn_bk': _L0_xattn_in['bk'], 'L0_xattn_Wv': _L0_xattn_in['Wv'], 'L0_xattn_bv': _L0_xattn_in['bv'], 'L0_xattn_Wo': _L0_xattn_in['Wo'], 'L0_xattn_bo': _L0_xattn_in['bo'], 'L0_ffn_gate_w': _L0_ffn_in['gate_w'], 'L0_ffn_gate_bias': _L0_ffn_in['gate_bias'], 'L0_ffn_Wu': _L0_ffn_in['Wu'], 'L0_ffn_bu': _L0_ffn_in['bu'], 'L0_ffn_Wd': _L0_ffn_in['Wd'], 'L0_ffn_bd': _L0_ffn_in['bd'], 'L0_ffn_sWu': _L0_ffn_in['sWu'], 'L0_ffn_sbu': _L0_ffn_in['sbu'], 'L0_ffn_sWd': _L0_ffn_in['sWd'], 'L0_ffn_sbd': _L0_ffn_in['sbd'], 'L1_xattn_ln_x_g': _L1_xattn_in['ln_x_g'], 'L1_xattn_ln_x_b': _L1_xattn_in['ln_x_b'], 'L1_xattn_ln_l_g': _L1_xattn_in['ln_l_g'], 'L1_xattn_ln_l_b': _L1_xattn_in['ln_l_b'], 'L1_xattn_qn_g': _L1_xattn_in['qn_g'], 'L1_xattn_kn_g': _L1_xattn_in['kn_g'], 'L1_xattn_Wq': _L1_xattn_in['Wq'], 'L1_xattn_Wkv': _L1_xattn_in['Wkv'], 'L1_xattn_Wlkv': _L1_xattn_in['Wlkv'], 'L1_xattn_Wo': _L1_xattn_in['Wo'], 'L1_xattn_bo': _L1_xattn_in['bo'], 'L1_ffn_gate_w': _L1_ffn_in['gate_w'], 'L1_ffn_gate_b': _L1_ffn_in['gate_b'], 'L1_ffn_expert_w': _L1_ffn_in['expert_w'], 'L1_ffn_expert_b': _L1_ffn_in['expert_b'], 'L2_xattn_Wq': _L2_xattn_in['Wq'], 'L2_xattn_bq': _L2_xattn_in['bq'], 'L2_xattn_Wk': _L2_xattn_in['Wk'], 'L2_xattn_bk': _L2_xattn_in['bk'], 'L2_xattn_Wv': _L2_xattn_in['Wv'], 'L2_xattn_bv': _L2_xattn_in['bv'], 'L2_xattn_Wo': _L2_xattn_in['Wo'], 'L2_xattn_bo': _L2_xattn_in['bo'], 'L2_xattn_ln_gamma': _L2_xattn_in['ln_gamma'], 'L2_xattn_ln_beta': _L2_xattn_in['ln_beta'], 'L2_ffn_Wg': _L2_ffn_in['Wg'], 'L2_ffn_bg': _L2_ffn_in['bg'], 'L2_ffn_Wu': _L2_ffn_in['Wu'], 'L2_ffn_bu': _L2_ffn_in['bu'], 'L2_ffn_Wd': _L2_ffn_in['Wd'], 'L2_ffn_bd': _L2_ffn_in['bd'], 'L2_ffn_Wq': _L2_ffn_in['Wq'], 'L2_ffn_keys': _L2_ffn_in['keys'], 'L2_ffn_down_embed': _L2_ffn_in['down_embed'], 'L2_ffn_up_embed': _L2_ffn_in['up_embed'], 'L3_xattn_Wq': _L3_xattn_in['Wq'], 'L3_xattn_Wk': _L3_xattn_in['Wk'], 'L3_xattn_Wv': _L3_xattn_in['Wv'], 'L3_xattn_Wo': _L3_xattn_in['Wo'], 'L3_xattn_bo': _L3_xattn_in['bo'], 'L3_ffn_W1': _L3_ffn_in['W1'], 'L3_ffn_b1': _L3_ffn_in['b1'], 'L3_ffn_W2': _L3_ffn_in['W2'], 'L3_ffn_b2': _L3_ffn_in['b2'], 'L3_ffn_Wr': _L3_ffn_in['Wr'], 'L3_ffn_br': _L3_ffn_in['br']}

def reference(x, ctx_768, mask_BxS2_bk0, g_xattn, g_ffn, L0_xattn_ln1_g, L0_xattn_ln1_b, L0_xattn_ln2_g, L0_xattn_ln2_b, L0_xattn_Wq, L0_xattn_bq, L0_xattn_Wk, L0_xattn_bk, L0_xattn_Wv, L0_xattn_bv, L0_xattn_Wo, L0_xattn_bo, L0_ffn_gate_w, L0_ffn_gate_bias, L0_ffn_Wu, L0_ffn_bu, L0_ffn_Wd, L0_ffn_bd, L0_ffn_sWu, L0_ffn_sbu, L0_ffn_sWd, L0_ffn_sbd, L1_xattn_ln_x_g, L1_xattn_ln_x_b, L1_xattn_ln_l_g, L1_xattn_ln_l_b, L1_xattn_qn_g, L1_xattn_kn_g, L1_xattn_Wq, L1_xattn_Wkv, L1_xattn_Wlkv, L1_xattn_Wo, L1_xattn_bo, L1_ffn_gate_w, L1_ffn_gate_b, L1_ffn_expert_w, L1_ffn_expert_b, L2_xattn_Wq, L2_xattn_bq, L2_xattn_Wk, L2_xattn_bk, L2_xattn_Wv, L2_xattn_bv, L2_xattn_Wo, L2_xattn_bo, L2_xattn_ln_gamma, L2_xattn_ln_beta, L2_ffn_Wg, L2_ffn_bg, L2_ffn_Wu, L2_ffn_bu, L2_ffn_Wd, L2_ffn_bd, L2_ffn_Wq, L2_ffn_keys, L2_ffn_down_embed, L2_ffn_up_embed, L3_xattn_Wq, L3_xattn_Wk, L3_xattn_Wv, L3_xattn_Wo, L3_xattn_bo, L3_ffn_W1, L3_ffn_b1, L3_ffn_W2, L3_ffn_b2, L3_ffn_Wr, L3_ffn_br):
    import jax
    import jax.numpy as jnp

    def _L0_xattn_ref(modality1, modality2, ln1_g, ln1_b, ln2_g, ln2_b, Wq, bq, Wk, bk, Wv, bv, Wo, bo):
        import jax, jax.numpy as jnp
        import numpy as np
        EPS = 1e-05

        def layernorm(x, g, b):
            mu = jnp.mean(x, axis=-1, keepdims=True)
            var = jnp.mean(jnp.square(x - mu), axis=-1, keepdims=True)
            return (x - mu) * jax.lax.rsqrt(var + EPS) * g + b
        E = Wq.shape[1]
        scaling = E ** (-0.5)
        x1 = layernorm(modality1, ln1_g, ln1_b)
        x2 = layernorm(modality2, ln2_g, ln2_b)
        q = x1 @ Wq + bq
        k = x2 @ Wk + bk
        v = x2 @ Wv + bv
        scores = jnp.einsum('bqe,bke->bqk', q, k) * scaling
        attn = jax.nn.softmax(scores, axis=-1)
        ctx = jnp.einsum('bqk,bke->bqe', attn, v)
        return ctx @ Wo + bo

    def _L0_ffn_ref(x, gate_w, gate_bias, Wu, bu, Wd, bd, sWu, sbu, sWd, sbd):
        import jax, jax.numpy as jnp
        import numpy as np
        B, S, H, E, K = (2, 256, 256, 8, 2)
        F = 4 * H
        b, s, h = x.shape
        x_flat = x.reshape(-1, h)
        T = x_flat.shape[0]
        scores = jax.nn.sigmoid(x_flat @ gate_w.T + gate_bias)
        top_scores, top_idx = jax.lax.top_k(scores, K)
        top_scores = top_scores / (top_scores.sum(-1, keepdims=True) + 1e-06)
        w = jnp.zeros((T, E), x.dtype).at[jnp.arange(T)[:, None], top_idx].add(top_scores)
        h1 = jnp.einsum('th,efh->etf', x_flat, Wu) + bu[:, None, :]
        a1 = jax.nn.gelu(h1, approximate=False)
        y = jnp.einsum('etf,ehf->eth', a1, Wd) + bd[:, None, :]
        combined = jnp.einsum('te,eth->th', w, y)
        sh = jax.nn.gelu(x_flat @ sWu.T + sbu, approximate=False)
        shared = (sh @ sWd.T + sbd) * 0.1
        return (combined + shared).reshape(b, s, h)

    def _L1_xattn_ref(x, latents, mask, ln_x_g, ln_x_b, ln_l_g, ln_l_b, qn_g, kn_g, Wq, Wkv, Wlkv, Wo, bo):
        import jax, jax.numpy as jnp
        import numpy as np
        DIM_IN, DIM_LAT, DIM_HEAD = (192, 256, 64)
        INNER = max(DIM_LAT, DIM_IN)
        HEADS = INNER // DIM_HEAD
        SCALE = DIM_HEAD ** (-0.5)
        RMS_EPS = 1e-08
        LN_EPS = 1e-05

        def layernorm(x, g, b):
            mu = jnp.mean(x, axis=-1, keepdims=True)
            var = jnp.mean((x - mu) ** 2, axis=-1, keepdims=True)
            return (x - mu) * jax.lax.rsqrt(var + LN_EPS) * g + b

        def rmsnorm(x, gamma):
            norm = jnp.sqrt(jnp.sum(x * x, axis=-1, keepdims=True)) * x.shape[-1] ** (-0.5)
            return x / jnp.maximum(norm, RMS_EPS) * gamma
        b, n, _ = x.shape
        m = latents.shape[1]
        xn = layernorm(x, ln_x_g, ln_x_b)
        ln = layernorm(latents, ln_l_g, ln_l_b)
        q = ln @ Wq.T
        kv = jnp.concatenate([xn @ Wkv.T, ln @ Wlkv.T], axis=1)
        k, v = (kv[..., :INNER], kv[..., INNER:])
        split_heads = lambda t: t.reshape(t.shape[0], t.shape[1], HEADS, DIM_HEAD).transpose(0, 2, 1, 3)
        q, k, v = (split_heads(q), split_heads(k), split_heads(v))
        qn = rmsnorm(q, qn_g) * SCALE
        kn = rmsnorm(k, kn_g)
        attn = jnp.einsum('bhid,bhjd->bhij', qn, kn)
        full_mask = jnp.pad(mask, ((0, 0), (0, m)), constant_values=True)
        attn = jnp.where(full_mask[:, None, None, :], attn, -jnp.finfo(attn.dtype).max)
        attn = jax.nn.softmax(attn, axis=-1)
        out = jnp.einsum('bhij,bhjd->bhid', attn, v)
        out = out.transpose(0, 2, 1, 3).reshape(b, m, INNER)
        return out @ Wo.T + bo

    def _L1_ffn_ref(x, gate_w, gate_b, expert_w, expert_b):
        import jax, jax.numpy as jnp
        import numpy as np
        TOP_K = 2
        gates = jax.nn.softmax(jnp.einsum('bsh,eh->bse', x, gate_w) + gate_b, axis=-1)
        top_gates, top_idx = jax.lax.top_k(gates, TOP_K)
        expert_out = jnp.einsum('bsh,eoh->bseo', x, expert_w) + expert_b
        selected = jnp.take_along_axis(expert_out, top_idx[..., None], axis=2)
        return (selected * top_gates[..., None]).sum(axis=2)

    def _L2_xattn_ref(query, key, value, Wq, bq, Wk, bk, Wv, bv, Wo, bo, ln_gamma, ln_beta):
        import jax, jax.numpy as jnp
        import numpy as np
        QUERY_DIM, KV_DIM, EMBED_DIM, NUM_HEADS = (256, 192, 256, 16)
        HEAD_DIM = EMBED_DIM // NUM_HEADS
        SCALE = HEAD_DIM ** (-0.5)
        LN_EPS = 1e-05

        def _l2norm(x, eps=1e-12):
            n = jnp.sqrt(jnp.sum(x * x, axis=-1, keepdims=True))
            return x / jnp.maximum(n, eps)
        B, Nq, _ = query.shape
        Nk = key.shape[1]
        Qp = query @ Wq + bq
        K = _l2norm(key @ Wk + bk)
        V = value @ Wv + bv
        Q = _l2norm(Qp)
        Q = Q.reshape(B, Nq, NUM_HEADS, HEAD_DIM).transpose(0, 2, 1, 3)
        K = K.reshape(B, Nk, NUM_HEADS, HEAD_DIM).transpose(0, 2, 1, 3)
        V = V.reshape(B, Nk, NUM_HEADS, HEAD_DIM).transpose(0, 2, 1, 3)
        scores = jnp.einsum('bhqd,bhkd->bhqk', Q, K) * SCALE
        attn = jax.nn.softmax(scores, axis=-1)
        out = jnp.einsum('bhqk,bhkd->bhqd', attn, V)
        out = out.transpose(0, 2, 1, 3).reshape(B, Nq, EMBED_DIM)
        out = out @ Wo + bo
        x = out + Qp
        mu = jnp.mean(x, axis=-1, keepdims=True)
        var = jnp.mean((x - mu) ** 2, axis=-1, keepdims=True)
        return (x - mu) / jnp.sqrt(var + LN_EPS) * ln_gamma + ln_beta

    def _L2_ffn_ref(hidden_states, Wg, bg, Wu, bu, Wd, bd, Wq, keys, down_embed, up_embed):
        import jax, jax.numpy as jnp
        import numpy as np
        B, T, D = (2, 512, 256)
        DCD = 1024
        RET = 128
        NEXP = 1024
        NKEYS = 64
        H = 4
        KPH = 8
        b, t, d = hidden_states.shape
        q = (hidden_states @ Wq).reshape(b, t, 2, H, RET // 2)
        sim = jnp.einsum('btphn,hkpn->pbthk', q, keys)
        sc, ix = jax.lax.top_k(sim, KPH)
        sx, sy = (sc[0], sc[1])
        ixx, ixy = (ix[0], ix[1])
        all_sc = (sx[..., :, None] + sy[..., None, :]).reshape(b, t, H, KPH * KPH)
        all_ix = (ixx[..., :, None] * NKEYS + ixy[..., None, :]).reshape(b, t, H, KPH * KPH)
        scores, pk = jax.lax.top_k(all_sc, KPH)
        idx = jnp.take_along_axis(all_ix, pk, axis=-1)
        de = down_embed[idx]
        ue = up_embed[idx]
        w = jnp.einsum('btd,bthkd->bthk', hidden_states, de)
        w = jax.nn.silu(w) * jax.nn.softmax(scores, axis=-1)
        experts_states = jnp.einsum('bthk,bthkd->btd', w, ue)
        mlp = jax.nn.silu(hidden_states @ Wg + bg) * (hidden_states @ Wu + bu) @ Wd + bd
        return mlp + experts_states

    def _L3_xattn_ref(x, context, Wq, Wk, Wv, Wo, bo):
        import jax, jax.numpy as jnp
        import numpy as np
        HEADS = 8
        DIM_HEAD = 64
        QUERY_DIM = 256
        CONTEXT_DIM = 192
        INNER = HEADS * DIM_HEAD
        B, Sq, _ = x.shape
        h, d = (HEADS, DIM_HEAD)
        scale = d ** (-0.5)
        q = (x @ Wq).reshape(B, Sq, h, d).transpose(0, 2, 1, 3)
        k = (context @ Wk).reshape(B, -1, h, d).transpose(0, 2, 1, 3)
        v = (context @ Wv).reshape(B, -1, h, d).transpose(0, 2, 1, 3)
        scores = jnp.einsum('bhid,bhjd->bhij', q, k) * scale
        attn = jax.nn.softmax(scores, axis=-1)
        out = jnp.einsum('bhij,bhjd->bhid', attn, v)
        out = out.transpose(0, 2, 1, 3).reshape(B, Sq, h * d)
        return out @ Wo + bo

    def _L3_ffn_ref(x, W1, b1, W2, b2, Wr, br):
        import jax, jax.numpy as jnp
        import numpy as np
        from jax import lax
        D = 256
        H = 1024
        E = 8
        TOPK = 2
        B, S, _ = x.shape
        xf = x.reshape(-1, D)
        logits = xf @ Wr + br
        topv, _ = lax.top_k(logits, TOPK)
        thresh = topv[:, TOPK - 1:TOPK]
        masked = jnp.where(logits >= thresh, logits, -jnp.inf)
        weights = jax.nn.softmax(masked, axis=-1)
        h = jax.nn.gelu(jnp.einsum('td,edh->eth', xf, W1) + b1[:, None, :], approximate=False)
        expert_out = jnp.einsum('eth,ehd->etd', h, W2) + b2[:, None, :]
        out = jnp.einsum('etd,te->td', expert_out, weights)
        return out.reshape(B, S, D)
    x = x + jnp.tanh(g_xattn[0]) * _L0_xattn_ref(_layernorm(x, axis=-1), ctx_768, L0_xattn_ln1_g, L0_xattn_ln1_b, L0_xattn_ln2_g, L0_xattn_ln2_b, L0_xattn_Wq, L0_xattn_bq, L0_xattn_Wk, L0_xattn_bk, L0_xattn_Wv, L0_xattn_bv, L0_xattn_Wo, L0_xattn_bo)
    x = x + jnp.tanh(g_ffn[0]) * _L0_ffn_ref(_layernorm(x, axis=-1), L0_ffn_gate_w, L0_ffn_gate_bias, L0_ffn_Wu, L0_ffn_bu, L0_ffn_Wd, L0_ffn_bd, L0_ffn_sWu, L0_ffn_sbu, L0_ffn_sWd, L0_ffn_sbd)
    x = x + jnp.tanh(g_xattn[1]) * _L1_xattn_ref(ctx_768, _layernorm(x, axis=-1), mask_BxS2_bk0, L1_xattn_ln_x_g, L1_xattn_ln_x_b, L1_xattn_ln_l_g, L1_xattn_ln_l_b, L1_xattn_qn_g, L1_xattn_kn_g, L1_xattn_Wq, L1_xattn_Wkv, L1_xattn_Wlkv, L1_xattn_Wo, L1_xattn_bo)
    x = x + jnp.tanh(g_ffn[1]) * _L1_ffn_ref(_layernorm(x, axis=-1), L1_ffn_gate_w, L1_ffn_gate_b, L1_ffn_expert_w, L1_ffn_expert_b)
    x = x + jnp.tanh(g_xattn[2]) * _L2_xattn_ref(_layernorm(x, axis=-1), ctx_768, ctx_768, L2_xattn_Wq, L2_xattn_bq, L2_xattn_Wk, L2_xattn_bk, L2_xattn_Wv, L2_xattn_bv, L2_xattn_Wo, L2_xattn_bo, L2_xattn_ln_gamma, L2_xattn_ln_beta)
    x = x + jnp.tanh(g_ffn[2]) * _L2_ffn_ref(_layernorm(x, axis=-1), L2_ffn_Wg, L2_ffn_bg, L2_ffn_Wu, L2_ffn_bu, L2_ffn_Wd, L2_ffn_bd, L2_ffn_Wq, L2_ffn_keys, L2_ffn_down_embed, L2_ffn_up_embed)
    x = x + jnp.tanh(g_xattn[3]) * _L3_xattn_ref(_layernorm(x, axis=-1), ctx_768, L3_xattn_Wq, L3_xattn_Wk, L3_xattn_Wv, L3_xattn_Wo, L3_xattn_bo)
    x = x + jnp.tanh(g_ffn[3]) * _L3_ffn_ref(_layernorm(x, axis=-1), L3_ffn_W1, L3_ffn_b1, L3_ffn_W2, L3_ffn_b2, L3_ffn_Wr, L3_ffn_br)
    return x

_drawn_inputs = setup_inputs


def setup_inputs(seed=0):
    import zlib

    import numpy as np

    out = dict(_drawn_inputs(seed))
    spreads = {'L0_xattn_ln1_g': (1.0, 0.2),
     'L0_xattn_ln1_b': (0.0, 0.289),
     'L0_xattn_ln2_g': (1.0, 0.2),
     'L0_xattn_ln2_b': (0.0, 0.1),
     'L0_ffn_gate_bias': (0.0, 0.1),
     'L0_ffn_bu': (0.0, 0.1),
     'L0_ffn_bd': (0.0, 0.1),
     'L0_ffn_sbu': (0.0, 0.711),
     'L0_ffn_sbd': (0.0, 0.4),
     'L1_xattn_ln_x_g': (1.0, 0.6),
     'L1_xattn_ln_x_b': (0.0, 0.8),
     'L1_xattn_ln_l_g': (1.0, 0.2),
     'L1_xattn_ln_l_b': (0.0, 0.1),
     'L1_xattn_qn_g': (1.0, 0.6),
     'L1_xattn_kn_g': (1.0, 0.6),
     'L1_xattn_bo': (0.0, 0.1),
     'L1_ffn_gate_b': (0.0, 0.1),
     'L1_ffn_expert_b': (0.0, 0.1),
     'L2_xattn_bq': (0.0, 0.1),
     'L2_xattn_bk': (0.0, 2.0),
     'L2_xattn_bv': (0.0, 0.1),
     'L2_xattn_bo': (0.0, 0.1),
     'L2_xattn_ln_gamma': (1.0, 0.2),
     'L2_xattn_ln_beta': (0.0, 0.1),
     'L2_ffn_bg': (0.0, 0.8),
     'L2_ffn_bu': (0.0, 0.8),
     'L2_ffn_bd': (0.0, 0.1),
     'L3_ffn_b1': (0.0, 0.569),
     'L3_ffn_b2': (0.0, 0.29),
     'L3_ffn_br': (0.0, 0.1)}
    factors = {'g_ffn': 33.384,
     'L0_xattn_bq': 8.0,
     'L0_xattn_bk': 64.0,
     'L0_xattn_bv': 3.098,
     'L0_xattn_bo': 3.693,
     'L0_ffn_sWu': 3.707,
     'L0_ffn_sWd': 3.933,
     'L1_xattn_Wkv': 4.026,
     'L2_xattn_Wk': 64.0,
     'L2_ffn_Wg': 3.029,
     'L2_ffn_Wu': 3.005,
     'L2_ffn_Wd': 2.875,
     'L2_ffn_Wq': 8.0,
     'L2_ffn_keys': 8.0,
     'L2_ffn_down_embed': 8.0,
     'L2_ffn_up_embed': 8.0,
     'L3_xattn_bo': 8.0}
    for name, (base, spread) in spreads.items():
        noise = np.random.default_rng([zlib.crc32(name.encode()), seed]).standard_normal(out[name].shape)
        drawn = base * np.exp(spread * noise) if base else spread * noise
        out[name] = jnp.asarray(drawn.astype(out[name].dtype))
    for name, factor in factors.items():
        out[name] = (out[name] * factor).astype(out[name].dtype)
    return out
```

```python
import concourse.bass as bass
from concourse import mybir
from concourse.alu_op_type import AluOpType as ALU
from contextlib import ExitStack
from collections import deque

F32 = mybir.dt.float32
F32R = mybir.dt.float32r
U32 = mybir.dt.uint32
U8 = mybir.dt.uint8
ACT = mybir.ActivationFunctionType
X_AXIS = mybir.AxisListType.X

P = 128
B, S, D = 2, 1024, 256
KC, DC = 77, 192
TILES = B * S // P
TPB = S // P
CT = 4
CHUNKS = TILES // CT
CTOK = CT * P
KD = D // P
EXPERTS = 8
SBUF_BYTES = 212800
BANK = 512
FLT_MAX = 3.4028234663852886e38
LN_EPS = 1e-5

WB = 2048
HALF = 512
L0_HALVES = (EXPERTS + 1) * 2
L3_HALVES = EXPERTS * 2
MLP_PARTS = 4
ITEMS = (["a0"] + [f"f0_{i}" for i in range(L0_HALVES)] + ["a1", "f1_0", "f1_1", "a2"]
         + [f"m2_{i}" for i in range(MLP_PARTS)] + ["pq", "pd", "pu", "a3"]
         + [f"f3_{i}" for i in range(L3_HALVES)])

COLS = {}
_n = 0
for _name, _k in (("ln1g", 2), ("ln1b", 2), ("ln2g", 2), ("ln2b", 2), ("bq0", 2), ("bk0", 2), ("bu0", 72),
                  ("lxg", 2), ("lxb", 2), ("llg", 2), ("llb", 2), ("qng", 1), ("kng", 1),
                  ("bg2", 8), ("bu2", 8), ("b13", 64), ("hm4", 4), ("hm2", 2)):
    COLS[_name] = (_n, _k)
    _n += _k
NCOLS = _n
ROWS = ["bo0", "bo1", "bd2", "bo3", "gamma2", "beta2", "bq2", "bo2"]
GATED_ROWS = {"bo0": 0, "bo1": 1, "bd2": 6, "bo3": 3, "gamma2": 2, "beta2": 2}
CTXROWS = ["bv0", "bk2", "bv2"]


class Queue:

    def __init__(self, semaphore):
        self.sem, self.count, self.todo, self.seen = semaphore, 0, [], {}

    def epoch(self, semaphore):
        self.sem, self.count = semaphore, 0

    def wait(self, after):
        for tok in after:
            if tok is None:
                continue
            if isinstance(tok, list):
                self.wait(tok)
                continue
            sem, value = tok
            if self.seen.get(id(sem), 0) < value:
                self.seen[id(sem)] = value
                self.todo.append(lambda e, s=sem, v=value: e.wait_ge(s, v))

    def add(self, build, after=(), signal=True):
        self.wait(after)
        if not signal:
            self.todo.append(build)
            return None
        self.count += 1
        self.todo.append(lambda e, s=self.sem: build(e).then_inc(s, 1))
        return (self.sem, self.count)

    def dma(self, out, in_, after, stream):
        self.wait(after)
        stream[1] += 16
        self.todo.append(lambda e, s=stream[0]: e.dma_start(out, in_).then_inc(s, 16))
        return (stream[0], stream[1])

    def copy(self, out, in_, after):
        return self.add(lambda e: e.tensor_copy(out, in_), after)

    def tt(self, out, a, b, op, after):
        return self.add(lambda e: e.tensor_tensor(out, a, b, op), after)

    def ts(self, out, a, s1, s2, op0, op1, after):
        if op1 is None:
            return self.add(lambda e: e.tensor_scalar(out, a, s1, None, op0), after)
        return self.add(lambda e: e.tensor_scalar(out, a, s1, s2, op0, op1), after)

    def stt(self, out, a, s, b, op0, op1, after):
        return self.add(lambda e: e.scalar_tensor_tensor(out, a, s, b, op0, op1), after)

    def reduce(self, out, a, op, after, negate=None):
        return self.add(lambda e: e.tensor_reduce(out, a, X_AXIS, op, negate=negate), after)

    def act(self, out, in_, func, after, bias=0.0, scale=1.0, accum=None):
        if accum is None:
            return self.add(lambda e: e.activation(out, in_, func, bias=bias, scale=scale), after)
        return self.add(lambda e: e.activation(out, in_, func, bias=bias, scale=scale, accum_out=accum), after)

    def memset(self, out, value, after=()):
        return self.add(lambda e: e.memset(out, value), after)

    def replay(self, engine):
        for build in self.todo:
            build(engine)


class Ring:
    job = 0

    def __init__(self, buffers):
        self.free = deque((b, []) for b in buffers)
        self.wanted = []

    def get(self):
        me = Ring.job
        self.wanted.append(me)
        while not self.free or min(self.wanted) != me:
            yield
        self.wanted.remove(me)
        return self.free.popleft()

    def give(self, buffer, *last):
        self.free.append((buffer, list(last)))


def interleave(jobs, background, window, queues):
    jobs, active, idle = deque(enumerate(jobs)), deque(), 0
    while jobs or active:
        while jobs and len(active) < window:
            active.append(jobs.popleft())
        before = (sum(len(q.todo) for q in queues), len(jobs))
        next(background, None)
        for number, job in list(active):
            Ring.job = number
            try:
                next(job)
            except StopIteration:
                active.remove((number, job))
        idle = 0 if before != (sum(len(q.todo) for q in queues), len(jobs)) else idle + 1
        assert idle < 20, "no job can go on: the order of the jobs is wrong"


def along(ap, axis, n):
    u = ap.unsqueeze(axis)
    shape = list(u.shape)
    shape[axis] = n
    return u.to_broadcast(shape)


def build_program(nc, A):
    ctx = ExitStack()
    with ctx:
        place = [0]

        def at(name, shape, dt, offset):
            return nc.alloc_sbuf_tensor_at(name, shape, dt, offset=offset)

        base = nc.sbuf_usable_end - SBUF_BYTES
        base = (base + 63) // 64 * 64

        def sb(name, shape, dt=F32):
            size = 4
            for k in shape[1:]:
                size *= k
            off = base + place[0]
            place[0] += (size + 31) // 32 * 32
            return at(name, shape, dt, off), off

        def sem(name):
            return ctx.enter_context(nc.semaphore(name))

        Xs = sb("X", [P, TILES, D])[0]
        XTh = sb("XT_hi", [P, KD, B * S], F32R)[0]
        XTl = sb("XT_lo", [P, KD, B * S], F32R)[0]
        w_slots = []
        for i in range(3):
            hi = sb(f"W{i}_hi", [P, WB], F32R)[0]
            lo, off = sb(f"W{i}_lo", [P, WB], F32R)
            w_slots.append((hi, lo, at(f"W{i}_raw", [P, WB], F32, off), [sem(f"w_load{i}"), 0]))
        h_slots, arena = [], None
        for i in range(2):
            hi, off = sb(f"H{i}_hi", [P, 4 * CTOK], F32R)
            arena = off if arena is None else arena
            h_slots.append((hi, sb(f"H{i}_lo", [P, 4 * CTOK], F32R)[0]))
        g_slots = [sb(f"G{i}", [P, CTOK])[0] for i in range(2)]
        NK1 = S + KC
        KT1 = at("KT1", [P, 2, B, NK1], F32, arena)
        V1 = at("V1", [P, B, TPB + 1, D], F32, arena + (2 * B * NK1 * 4 + 31) // 32 * 32)
        arena1 = arena + (2 * B * NK1 * 4 + 31) // 32 * 32 + B * (TPB + 1) * D * 4
        assert arena1 <= arena + 4 * 8192 + 2 * 2048
        KT2, off = sb("KT2", [P, 2, B, 4, KC])
        V2 = sb("V2", [KC, B, 8, 2, 32])[0]
        SCR = at("SCR", [P, 2048], F32, off)
        KT3 = sb("KT3", [P, 4, B, 2, KC])[0]
        V3 = sb("V3", [KC, B, 512])[0]
        kT0, off = sb("kT0", [P, 2, B, KC])
        V0 = sb("V0", [KC, B, D])[0]
        KEYS = at("KEYS", [P, 4, P], F32, off)
        p_slots = [sb(f"P{i}", [P, 16 * KC])[0] for i in range(3)]
        pt_slots = [sb(f"PT{i}", [P, BANK])[0] for i in range(6)]
        OTh = sb("OT_hi", [P, 4 * P], F32R)[0]
        OTl = sb("OT_lo", [P, 4 * P], F32R)[0]
        SIM, off = sb("SIM", [P, 8, 64])
        GRID = sb("GRID", [P, 2, 256])[0]
        EXB = sb("EXB", [P, 64 + 256 + 32])[0]
        ctx_raw = at("ctx_raw", [KC, B, DC], F32, off)
        ctxT = [at(f"ctxT{i}", [P, 2, B * KC], F32, off + B * DC * 4 + i * 1248) for i in range(3)]
        assert 2 * B * KC * 4 <= 1248 and B * DC * 4 + 3 * 1248 <= (512 + 512 + 352) * 4
        rows = sb("rows", [P, len(ROWS), D])[0]
        cols = sb("cols", [P, NCOLS])[0]
        ident = sb("ident", [P, P])[0]
        tg = sb("tg", [P, 8])[0]
        half = sb("half", [P, 8])[0]
        iota = sb("iota", [P, 64])[0]
        rank8 = sb("rank8", [P, 8])[0]
        gbias = sb("gbias", [P, 3, EXPERTS])[0]
        gateh = sb("gate_hi", [P, 3, KD, EXPERTS], F32R)[0]
        gatel, off = sb("gate_lo", [P, 3, KD, EXPERTS], F32R)
        gater = at("gate_raw", [P, 3, KD, EXPERTS], F32, off)
        bdown = sb("bdown", [EXPERTS + 1, D])[0]
        maskf = sb("maskf", [P, B, KC])[0]
        maskn = sb("maskn", [P, B, KC])[0]
        RW = sb("RW", [P, CHUNKS, CT, EXPERTS + 1])[0]
        small = sb("small", [P, 8, 32])[0]
        mask8, off = sb("mask8", [P, B * KC // 4 + 4])
        mask8 = at("mask8b", [P, B, KC], U8, off)
        st6 = sb("st6", [P, 2, CT, 6])[0]
        mv = sb("mv", [P, 2, CT, 2])[0]
        rs = sb("rs", [P, 2, CT])[0]
        tiny = sb("tiny", [P, 4, 48])[0]
        V8 = sb("V8", [P, 8, 8])[0]
        I8 = sb("I8", [P, 8, 8], U32)[0]
        I8f = sb("I8f", [P, 8, 8])[0]
        T8 = sb("T8", [P, 4, 8])[0]
        CX = sb("CX", [P, 4, 16])[0]
        RY = sb("RY", [P, 4, 64])[0]
        CA = sb("CA", [P, 4, 8])[0]
        pz = sb("pz", [P, 16])[0]
        assert place[0] <= SBUF_BYTES - 64

        banks = [ctx.enter_context(nc.psum_tensor(f"bank{i}", [P, BANK], F32)) for i in range(8)]
        bank = Ring(banks)
        w_ring, h_ring, g_ring = Ring(w_slots), Ring(h_slots), Ring(g_slots)
        p_ring, pt_ring = Ring(p_slots), Ring(pt_slots)
        tiny_ring = Ring([tiny[:, i, :] for i in range(4)])
        ln_ring = Ring([0, 1])
        ot_ring = Ring([(OTh, OTl)])
        sim_ring, scratch_ring = Ring([SIM]), Ring(["scratch"])
        attention_ring, attention1_ring, head_ring = Ring(range(3)), Ring(range(2)), Ring(range(3))

        PE, AC, DV, PL, SY = (Queue(sem(f"{n}_load")) for n in ("pe", "act", "dve", "pool", "sync"))

        T = {}

        def last_of(key, n, tok):
            T[key, "count"] = T.get((key, "count"), 0) + 1
            if T[key, "count"] == n:
                T[key] = tok

        def until(key):
            while key not in T:
                yield
            return T[key]

        def col(name, i=0, rows_=P):
            return cols[0:rows_, COLS[name][0] + i:COLS[name][0] + i + 1]

        def row(name, rows_=P):
            return rows[0:rows_, ROWS.index(name), :]

        s_const = [sem("const_load"), 0]
        s_x = [[sem(f"x_load{c}"), 0] for c in range(CHUNKS)]
        s_out = [sem("out_store"), 0]
        s_ctx = [sem("ctx_load"), 0]
        s_bv0 = [sem("bv0_load"), 0]
        s_bkv2 = [sem("bkv2_load"), 0]
        s_bdown = [sem("bdown_load"), 0]
        s_keys = [sem("keys_load"), 0]
        xv = A["x"].rearrange("b (n p) d -> p (b n) d", p=P)
        for c in range(CHUNKS):
            t = SY.dma(Xs[:, c * CT:(c + 1) * CT, :], xv[:, c * CT:(c + 1) * CT, :], (), s_x[c])
            for i in range(c * CT, (c + 1) * CT):
                T["x", i] = t
        for dst, src in ((cols[:, :], A["cols"]), (ident[:, :], A["ident"]), (iota[:, :], A["iota"]),
                         (rank8[:, :], A["rank8"]),
                         (gater[:, :, :, :].rearrange("p a b c -> p (a b c)"), A["gates"]),
                         (tg[:, :], A["g"].partition_broadcast(P)),
                         (gbias[:, :, :].rearrange("p a b -> p (a b)"), A["gbias"].partition_broadcast(P)),
                         (rows[:, :, :].rearrange("p a b -> p (a b)"), A["rows"].partition_broadcast(P)),
                         (mask8[:, :, :].rearrange("p a b -> p (a b)"), A["mask"].partition_broadcast(P))):
            loaded = SY.dma(dst, src, (), s_const)
        t_half = PL.memset(half[:, 0:4], -0.5)
        t_half = PL.memset(half[:, 4:8], 0.5)
        t_tg = AC.act(tg[:, :], tg[:, :], ACT.Tanh, [loaded])
        for name, g in GATED_ROWS.items():
            t_rows = DV.ts(row(name), row(name), tg[:, g:g + 1], None, ALU.mult, None, [loaded, t_tg])
        t_m = DV.copy(maskf[:, :, :], mask8[:, :, :], [loaded])
        t_m = DV.ts(maskn[:, :, :], maskf[:, :, :], -1.0, FLT_MAX, ALU.add, ALU.mult, [t_m])
        t_gh = PL.copy(gateh[:, :, :, :], gater[:, :, :, :], [loaded])
        t_g = DV.tt(gatel[:, :, :, :], gater[:, :, :, :], gateh[:, :, :, :].bitcast(F32), ALU.subtract, [t_gh])
        t_gate = [t_gh, t_g]

        USES = {}
        for n in ITEMS:
            USES[n] = CHUNKS if n[0] in "fm" else TILES

        class Block:
            def __init__(self, slot, ready, uses):
                self.hi, self.lo, self.slot, self.ready, self.uses = slot[0], slot[1], slot, ready, uses

            def done(self, tok):
                self.uses -= 1
                if self.uses == 0:
                    w_ring.give(self.slot, tok)

        def weights_job():
            waiting = deque()
            for n, name in enumerate(ITEMS):
                while not w_ring.free:
                    yield
                    yield from flush(waiting)
                slot, last = w_ring.free.popleft()
                loaded = SY.dma(slot[2][:, :], A["blocks"][n], last, slot[3])
                waiting.append([2, name, slot, loaded])
                yield from flush(waiting)
            while waiting:
                yield
                yield from flush(waiting)

        def flush(waiting):
            for w in waiting:
                w[0] -= 1
            while waiting and waiting[0][0] <= 0:
                _, name, slot, loaded = waiting.popleft()
                hi, lo, raw, _ = slot
                a = PL.copy(hi[:, :], raw[:, :], [loaded])
                b = DV.tt(lo[:, :], raw[:, :], hi[:, :].bitcast(F32), ALU.subtract, [a])
                T["w", name] = Block(slot, [a, b], USES[name])
            return
            yield

        def mm3(out, lhs, rhs, first, last, after=()):
            PE.wait(after)
            (lh, ll), (rh, rl) = lhs, rhs
            tok = None
            for i, (a, b) in enumerate(((lh, rh), (lh, rl), (ll, rh))):
                f, z = first and i == 0, last and i == 2
                tok = PE.add(lambda e, a=a, b=b, f=f, z=z: e.matmul(out, a, b, start=f, stop=z), signal=z)
            return tok

        def mm(out, lhs, rhs, first, last, after=(), signal=None):
            return PE.add(lambda e: e.matmul(out, lhs, rhs, start=first, stop=last), after,
                          signal=last if signal is None else signal)

        def transpose(out, in_, after=(), signal=True):
            n = in_.shape[0]
            return PE.add(lambda e: e.transpose(out, in_, ident[0:n, 0:n]), after, signal=signal)

        def split(src, hi, lo, after, war):
            a = PL.copy(hi, src, [after, war])
            b = DV.tt(lo, src, hi.bitcast(F32), ALU.subtract, [after, a, war])
            return [a, b]

        def normalize(src, dst, n, width, parts, after, war, st):
            last = []
            for i in range(n):
                last.append(DV.add(lambda e, i=i: e.bn_stats(st6[0:parts, st, i, :], src(i)), [after[i], war]))
            for i in range(n):
                tok = DV.add(lambda e, i=i: e.bn_aggr(mv[0:parts, st, i, :], st6[0:parts, st, i, :]), [last[i]])
            e1 = DV.ts(rs[0:parts, st, 0:n], mv[0:parts, st, 0:n, 1], LN_EPS, None, ALU.add, None, [tok])
            e2 = PL.tt(rs[0:parts, st, 0:n], rs[0:parts, st, 0:n], half[0:parts, 0:n], ALU.pow, [e1, t_half])
            out = []
            for i in range(n):
                out.append(DV.ts(dst(i), src(i), mv[0:parts, st, i, 0:1], rs[0:parts, st, i:i + 1],
                                 ALU.subtract, ALU.mult, [e2, war]))
            return out

        def tokens_job(key, c, gain=None, second=False):
            for i in range(CT):
                yield from until(("x_ready", key, c * CT + i))
            xn, war = yield from p_ring.get()
            xn3 = xn[:, 0:CT * D].rearrange("p (t d) -> p t d", t=CT)
            st, warst = yield from ln_ring.get()
            toks = normalize(lambda i: Xs[:, c * CT + i, :], lambda i: xn3[:, i, :], CT, D, P,
                             [T["x", c * CT + i] for i in range(CT)], [war, warst], st)
            for i in range(CT):
                T["x_read", key, c * CT + i] = toks[i]
            yield
            if second:
                toks = normalize(lambda i: xn3[:, i, :], lambda i: xn3[:, i, :], CT, D, P, toks, [], st)
                yield
            ln_ring.give(st, toks[-1])
            free = [T["xt_last", key - 1, c]] if key > 0 else []
            out = []
            for k in range(KD):
                ps, pw = yield from bank.get()
                for i in range(CT):
                    t = transpose(ps[:, i * P:(i + 1) * P], xn3[:, i, k * P:(k + 1) * P],
                                  [toks[i], pw, loaded], signal=i == CT - 1)
                y, yw = yield from pt_ring.get()
                kw = dict(scale=col(gain[0], k), bias=col(gain[1], k)) if gain else {}
                a = AC.act(y[:, :], ps[:, :], ACT.Identity, [t, yw, loaded], **kw)
                bank.give(ps, a)
                o = split(y[:, :], XTh[:, k, c * CTOK:(c + 1) * CTOK], XTl[:, k, c * CTOK:(c + 1) * CTOK], a, free)
                pt_ring.give(y, *o)
                out += o
            p_ring.give(xn, t)
            T["xt", key, c] = out
            yield

        def xt(k, lo, hi):
            return (XTh[:, k, lo:hi], XTl[:, k, lo:hi])

        def wv(block, a, b):
            return (block.hi[:, a:b], block.lo[:, a:b])


        def ctx_job():
            t_in = SY.dma(ctx_raw[:, :, :], A["ctx"].rearrange("b k d -> k b d"), (), s_ctx)
            def transposes(gains, after):
                ps, pw = yield from bank.get()
                for k, n in ((0, P), (1, DC - P)):
                    for b in range(B):
                        t = transpose(ps[0:n, (k * B + b) * KC:(k * B + b + 1) * KC],
                                      ctx_raw[:, b, k * P:k * P + n], [after, pw, loaded], signal=True)
                out = []
                for dst, g in gains:
                    for k, n in ((0, P), (1, DC - P)):
                        kw = dict(scale=col(g[0], k, n), bias=col(g[1], k, n)) if g else {}
                        out.append(AC.act(dst[0:n, k, :], ps[0:n, k * B * KC:(k + 1) * B * KC],
                                          ACT.Identity, [t], **kw))
                bank.give(ps, out[-1])
                return out
            raw = yield from transposes([(ctxT[0], None)], t_in)
            yield
            st, warst = yield from ln_ring.get()
            toks = normalize(lambda i: ctx_raw[:, i, :], lambda i: ctx_raw[:, i, :], B, DC, KC,
                             [t_in] * B, [warst, raw], st)
            ln_ring.give(st, toks[-1])
            yield
            T["ctx"] = raw + (yield from transposes([(ctxT[1], ("ln2g", "ln2b")), (ctxT[2], ("lxg", "lxb"))], toks[-1:]))

        def ctx_weights(name, after):
            w, war = yield from p_ring.get()
            w3 = w[:, 0:1024].rearrange("p (k n) -> p k n", k=2)
            stream = [sem(f"{name}_load"), 0]
            a = SY.dma(w3[:, 0, :], A[name][0:P, :], [war, after], stream)
            b = SY.dma(w3[0:DC - P, 1, :], A[name][P:DC, :], [war, after], stream)
            return w, w3, b

        def ctx0_job():
            w, w3, tw = yield from ctx_weights("ctxw0", None)
            r, war = yield from pt_ring.get()
            tr = SY.dma(r[0:KC, 0:D], A["ctxrows"][0:1, :].rearrange("a d -> (a d)").partition_broadcast(KC), war, s_bv0)
            yield
            cready = yield from until("ctx")
            out = []
            for e in range(2):
                ps, pw = yield from bank.get()
                for k, n in ((0, P), (1, DC - P)):
                    t = mm(ps[:, 0:B * KC], w3[0:n, k, e * P:(e + 1) * P], ctxT[1][0:n, k, :], k == 0, k == 1,
                           [tw, pw, cready])
                a = AC.act(kT0[:, e, :, :].rearrange("p b k -> p (b k)"), ps[:, 0:B * KC], ACT.Identity, [t],
                           bias=col("bk0", e))
                bank.give(ps, a)
                out.append(a)
            for b in range(B):
                ps, pw = yield from bank.get()
                for k, n in ((0, P), (1, DC - P)):
                    t = mm(ps[0:KC, 0:D], ctxT[1][0:n, k, b * KC:(b + 1) * KC], w3[0:n, k, D:2 * D], k == 0, k == 1, [pw])
                a = DV.tt(V0[:, b, :], ps[0:KC, 0:D], r[0:KC, 0:D], ALU.add, [t, tr])
                bank.give(ps, a)
                out.append(a)
            p_ring.give(w, t)
            pt_ring.give(r, a)
            T["kv0"] = out

        def ctx2_job():
            w, w3, tw = yield from ctx_weights("ctxw2", None)
            r, war = yield from pt_ring.get()
            tr = SY.dma(r[0:KC, :], A["ctxrows"][1:3, :].rearrange("a d -> (a d)").partition_broadcast(KC), war, s_bkv2)
            yield
            z = PL.memset(V2[:, :, :, :, :], 0.0)
            out = []
            for b in range(B):
                ps, pw = yield from bank.get()
                for k, n in ((0, P), (1, DC - P)):
                    t = mm(ps[0:KC, :], ctxT[0][0:n, k, b * KC:(b + 1) * KC], w3[0:n, k, :], k == 0, k == 1, [tw, pw])
                kv, war = yield from pt_ring.get()
                a = DV.tt(kv[0:KC, :], ps[0:KC, :], r[0:KC, :], ALU.add, [t, tr, war])
                bank.give(ps, a)
                vv = kv[0:KC, D:2 * D].rearrange("p (q two d) -> p q two d", two=2, d=16)
                for j in range(2):
                    out.append(AC.act(V2[:, b, :, j, 16 * j:16 * j + 16], vv[:, :, j, :], ACT.Copy, [a, z]))
                tn, war = yield from tiny_ring.get()
                sq, war2 = yield from pt_ring.get()
                s = AC.act(sq[0:KC, 0:D], kv[0:KC, 0:D], ACT.Square, [a, war, war2], accum=tn[0:KC, 0:1])
                s = PL.tt(tn[0:KC, 0:1], tn[0:KC, 0:1], half[0:KC, 4:5], ALU.pow, [s])
                s = DV.ts(tn[0:KC, 0:1], tn[0:KC, 0:1], 1e-12, None, ALU.max, None, [s])
                s = DV.add(lambda e, tn=tn: e.reciprocal(tn[0:KC, 1:2], tn[0:KC, 0:1]), [s])
                s = DV.ts(sq[0:KC, 0:D], kv[0:KC, 0:D], tn[0:KC, 1:2], None, ALU.mult, None, [s])
                tiny_ring.give(tn, s)
                ps, pw = yield from bank.get()
                for e in range(2):
                    t = transpose(ps[:, e * KC:(e + 1) * KC], sq[0:KC, e * P:(e + 1) * P], [s, pw])
                pt_ring.give(sq, t)
                pt_ring.give(kv, s, out[-1])
                for e in range(2):
                    for h in range(4):
                        a = DV.ts(KT2[:, e, b, h, :], ps[:, e * KC:(e + 1) * KC], col("hm4", h), None, ALU.mult, None, [t])
                out.append(a)
                bank.give(ps, a)
                yield
            p_ring.give(w, t)
            pt_ring.give(r, a)
            T["kv2"] = out

        def ctx3_job():
            yield from until("kv2")
            out = []
            for part in range(2):
                w, w3, tw = yield from ctx_weights(f"ctxw3{'kv'[part]}", None)
                yield
                if part == 0:
                    for e in range(4):
                        ps, pw = yield from bank.get()
                        for k, n in ((0, P), (1, DC - P)):
                            t = mm(ps[:, 0:B * KC], w3[0:n, k, e * P:(e + 1) * P], ctxT[0][0:n, k, :], k == 0, k == 1,
                                   [tw, pw])
                        pv = ps[:, 0:B * KC].rearrange("p (b k) -> p b k", b=B)
                        for h in range(2):
                            a = DV.ts(KT3[:, e, :, h, :], pv, col("hm2", h), None, ALU.mult, None, [t])
                        bank.give(ps, a)
                        out.append(a)
                else:
                    for b in range(B):
                        ps, pw = yield from bank.get()
                        for k, n in ((0, P), (1, DC - P)):
                            t = mm(ps[0:KC, :], ctxT[0][0:n, k, b * KC:(b + 1) * KC], w3[0:n, k, :], k == 0, k == 1,
                                   [tw, pw])
                        a = AC.act(V3[:, b, :], ps[0:KC, :], ACT.Copy, [t])
                        bank.give(ps, a)
                        out.append(a)
                p_ring.give(w, t)
                yield
            T["kv3"] = out

        HEADS = {0: 1, 2: 16, 3: 8}
        EDIM = {0: 256, 2: 256, 3: 512}

        def residual(tile, ps, layer, after):
            a = PL.tt(Xs[:, tile, :], Xs[:, tile, :], row(f"bo{layer}"), ALU.add,
                      [T["x_read", 2 * layer, tile], T["x", tile], t_rows])
            return DV.stt(Xs[:, tile, :], ps, tg[:, layer:layer + 1], Xs[:, tile, :], ALU.mult, ALU.add, [a, after])

        def project_out(ot, tps, nE, wblock, w_at, war):
            hi, lo = ot
            y, yw = yield from pt_ring.get()
            a = AC.act(y[:, 0:nE * P], tps[0][:, 0:nE * P], ACT.Copy, [tps[1], yw])
            bank.give(tps[0], a)
            o = split(y[:, 0:nE * P], hi[:, 0:nE * P], lo[:, 0:nE * P], a, war)
            pt_ring.give(y, *o)
            yield
            ps, pw = yield from bank.get()
            for e in range(nE):
                t = mm3(ps[:, 0:D], (hi[:, e * P:(e + 1) * P], lo[:, e * P:(e + 1) * P]),
                        wv(wblock, w_at + e * D, w_at + (e + 1) * D), e == 0, e == nE - 1, [o, pw, wblock.ready])
            return ps, t

        def attention_job(layer, tile):
            b, nH, E, key = tile // TPB, HEADS[layer], EDIM[layer], 2 * layer
            nE = E // P
            ticket, _ = yield from attention_ring.get()
            yield from until(("xt", key, tile // CT))
            w = yield from until(("w", f"a{layer}"))
            kv = yield from until(f"kv{layer}")
            t0 = tile * P
            ps, pw = yield from bank.get()
            for k in range(KD):
                t = mm3(ps[:, 0:E], xt(k, t0, t0 + P), wv(w, k * E, (k + 1) * E), k == 0, k == KD - 1,
                        [T["xt", key, tile // CT], w.ready, pw])
            T["xt_last", key, tile // CT] = t
            qs, war = yield from pt_ring.get()
            tn, war2 = yield from tiny_ring.get()
            if layer == 2:
                t = DV.tt(qs[:, 0:E], ps[:, 0:E], row("bq2"), ALU.add, [t, war])
                bank.give(ps, t)
                s = AC.act(qs[:, E:2 * E], qs[:, 0:E], ACT.Square, [t, war2], accum=tn[:, 16:17])
                s = PL.tt(tn[:, 16:17], tn[:, 16:17], half[:, 4:5], ALU.pow, [s])
                s = DV.ts(tn[:, 16:17], tn[:, 16:17], 1e-12, None, ALU.max, None, [s])
                s = DV.add(lambda e: e.reciprocal(tn[:, 17:18], tn[:, 16:17]), [s])
                scale_ready = DV.ts(tn[:, 17:18], tn[:, 17:18], 0.25, None, ALU.mult, None, [s])
            else:
                t = AC.act(qs[:, 0:E], ps[:, 0:E], ACT.Copy, [t, war])
                bank.give(ps, t)
            yield
            ps, pw = yield from bank.get()
            for e in range(nE):
                tq = transpose(ps[:, e * P:(e + 1) * P], qs[:, e * P:(e + 1) * P], [t, pw])
            if layer != 2:
                pt_ring.give(qs, tq)
            qT, war = yield from pt_ring.get()
            if layer == 0:
                for e in range(nE):
                    t = DV.ts(qT[:, e * P:(e + 1) * P], ps[:, e * P:(e + 1) * P], col("bq0", e), D ** -0.5,
                              ALU.add, ALU.mult, [tq, war])
            else:
                t = AC.act(qT[:, 0:E], ps[:, 0:E], ACT.Copy, [tq, war], scale=1.0 if layer == 2 else 0.125)
            bank.give(ps, t)
            yield
            pb, war = yield from p_ring.get()
            if layer == 2:
                for g in range(4):
                    ps, pw = yield from bank.get()
                    lo = 64 * (g % 2)
                    ts_ = mm(ps[:, 0:4 * KC], qT[lo:lo + 64, (g // 2) * P:(g // 2 + 1) * P],
                             KT2[lo:lo + 64, g // 2, b, :, :].rearrange("p h k -> p (h k)"), True, True, [t, kv, pw])
                    a = AC.act(pb[:, g * 4 * KC:(g + 1) * 4 * KC], ps[:, 0:4 * KC], ACT.Exp,
                               [ts_, war, scale_ready], scale=tn[:, 17:18])
                    bank.give(ps, a)
            elif layer == 3:
                for g in range(2):
                    ps, pw = yield from bank.get()
                    for j in range(2):
                        e = 2 * g + j
                        ts_ = mm(ps[:, 2 * j * KC:2 * (j + 1) * KC], qT[:, e * P:(e + 1) * P],
                                 KT3[:, e, b, :, :].rearrange("p h k -> p (h k)"), True, True, [t, kv, pw])
                    pv = ps[:, 0:4 * KC].rearrange("p (h k) -> p h k", k=KC)
                    m = DV.reduce(tn[:, 20 + 4 * g:24 + 4 * g], pv, ALU.max, [ts_, war2])
                    a = DV.tt(pb[:, g * 4 * KC:(g + 1) * 4 * KC].rearrange("p (h k) -> p h k", k=KC), pv,
                              along(tn[:, 20 + 4 * g:24 + 4 * g], 2, KC), ALU.subtract, [m, war])
                    bank.give(ps, a)
                a = AC.act(pb[:, 0:nH * KC], pb[:, 0:nH * KC], ACT.Exp, [a])
            else:
                ps, pw = yield from bank.get()
                for e in range(2):
                    ts_ = mm(ps[:, 0:KC], qT[:, e * P:(e + 1) * P], kT0[:, e, b, :], e == 0, e == 1, [t, kv, pw])
                m = DV.reduce(tn[:, 20:21], ps[:, 0:KC], ALU.max, [ts_, war2], negate=True)
                a = AC.act(pb[:, 0:KC], ps[:, 0:KC], ACT.Exp, [m, war], bias=tn[:, 20:21])
                bank.give(ps, a)
            pt_ring.give(qT, ts_)
            yield
            p3 = pb[:, 0:nH * KC].rearrange("p (h k) -> p h k", k=KC)
            s = DV.reduce(tn[:, 0:nH], p3, ALU.add, [a, war2])
            s = DV.add(lambda e: e.reciprocal(tn[:, 28:28 + nH], tn[:, 0:nH]), [s])
            if nH == 1:
                a = DV.ts(pb[:, 0:KC], pb[:, 0:KC], tn[:, 28:29], None, ALU.mult, None, [s])
            else:
                a = DV.tt(p3, p3, along(tn[:, 28:28 + nH], 2, KC), ALU.mult, [s])
            tiny_ring.give(tn, a)
            yield
            ops, opw = yield from bank.get()
            for g in range(0, nH, 4):
                ps, pw = yield from bank.get()
                n = min(4, nH)
                for h in range(n):
                    t = transpose(ps[0:KC, h * P:(h + 1) * P], pb[:, (g + h) * KC:(g + h + 1) * KC], [a, pw],
                                  signal=h == n - 1)
                pT, war = yield from pt_ring.get()
                if g // 4 % 2:
                    cp = DV.copy(pT[0:KC, 0:n * P], ps[0:KC, 0:n * P], [t, war])
                else:
                    cp = AC.act(pT[0:KC, 0:n * P], ps[0:KC, 0:n * P], ACT.Copy, [t, war])
                bank.give(ps, cp)
                yield
                if layer == 0:
                    for e in range(2):
                        to = mm(ops[:, e * P:(e + 1) * P], V0[:, b, e * P:(e + 1) * P], pT[0:KC, 0:P], True, True,
                                [cp, opw])
                elif layer == 2:
                    for h in range(n):
                        hh = g + h
                        q4, e = hh // 2 % 4, hh // 8
                        to = mm(ops[32 * q4:32 * q4 + 32, e * P:(e + 1) * P], V2[:, b, hh // 2, hh % 2, :],
                                pT[0:KC, h * P:(h + 1) * P], hh % 2 == 0, hh % 2 == 1, [cp, opw])
                else:
                    for h in range(n):
                        hh = g + h
                        to = mm(ops[64 * (hh % 2):64 * (hh % 2) + 64, (hh // 2) * P:(hh // 2 + 1) * P],
                                V3[:, b, hh * 64:(hh + 1) * 64], pT[0:KC, h * P:(h + 1) * P], True, True, [cp, opw])
                pt_ring.give(pT, to)
            p_ring.give(pb, t)
            if layer == 2:
                last_of("kv2_done", TILES, to)
            ot, war = yield from ot_ring.get()
            ps, t = yield from project_out(ot, (ops, to), nE, w, KD * E, war)
            ot_ring.give(ot, t)
            w.done(t)
            if layer == 2:
                z, war = yield from pt_ring.get()
                a = DV.tt(z[:, 0:D], ps[:, 0:D], qs[:, 0:D], ALU.add, [t, war])
                bank.give(ps, a)
                pt_ring.give(qs, a)
                a = PL.tt(z[:, 0:D], z[:, 0:D], row("bo2"), ALU.add, [a])
                yield
                st, warst = yield from ln_ring.get()
                a = normalize(lambda i: z[:, 0:D], lambda i: z[:, D:2 * D], 1, D, P, [a], warst, st)
                ln_ring.give(st, a[0])
                a = DV.tt(z[:, 0:D], z[:, D:2 * D], row("gamma2"), ALU.mult, [a[0], t_rows])
                a2 = PL.tt(z[:, 0:D], z[:, 0:D], row("beta2"), ALU.add, [a])
                a = PL.tt(Xs[:, tile, :], Xs[:, tile, :], z[:, 0:D], ALU.add, [a2, T["x_read", key, tile], T["x", tile]])
                pt_ring.give(z, a)
            else:
                a = residual(tile, ps[:, 0:D], layer, t)
                bank.give(ps, a)
            T["x", tile] = a
            T["x_ready", key + 1, tile] = a
            attention_ring.give(ticket)
            yield

        def rms_scale(sq, src, n, parts, tn, after, war):
            a = AC.act(sq[0:parts, 0:n * 64], src, ACT.Square, [after, war])
            a = DV.reduce(tn[0:parts, 0:n], sq[0:parts, 0:n * 64].rearrange("p (h d) -> p h d", d=64), ALU.add, [a])
            a = PL.tt(tn[0:parts, 0:n], tn[0:parts, 0:n], half[0:parts, 4:4 + n], ALU.pow, [a])
            a = DV.ts(tn[0:parts, 0:n], tn[0:parts, 0:n], 0.125, 1e-8, ALU.mult, ALU.max, [a])
            return DV.add(lambda e: e.reciprocal(tn[0:parts, n:2 * n], tn[0:parts, 0:n]), [a])

        def key_tail(ps, t, parts, b, key0, vslot):
            v = AC.act(V1[0:parts, b, vslot, :], ps[0:parts, D:2 * D], ACT.Copy, [t, T["h_done0"]])
            kn, war = yield from pt_ring.get()
            tn, war2 = yield from tiny_ring.get()
            s = rms_scale(kn, ps[0:parts, 0:D], 4, parts, tn, t, [war, war2])
            s = DV.tt(kn[0:parts, 0:D].rearrange("p (h d) -> p h d", d=64),
                      ps[0:parts, 0:D].rearrange("p (h d) -> p h d", d=64),
                      along(tn[0:parts, 4:8], 2, 64), ALU.mult, [s])
            bank.give(ps, s, v)
            tiny_ring.give(tn, s)
            yield
            ps, pw = yield from bank.get()
            for e in range(2):
                t = transpose(ps[:, e * P:e * P + parts], kn[0:parts, e * P:(e + 1) * P], [s, pw])
            pt_ring.give(kn, t)
            a = AC.act(KT1[:, :, b, key0:key0 + parts],
                       ps[:, 0:2 * P].rearrange("p (e k) -> p e k", e=2)[:, :, 0:parts], ACT.Copy,
                       [t, T["h_done0"]], scale=col("kng"))
            bank.give(ps, a)
            return [v, a]

        def keys1_ctx_job():
            w, w3, tw = yield from ctx_weights("ctxw1", None)
            yield from until("h_done0")
            for b in range(B):
                ps, pw = yield from bank.get()
                for k, n in ((0, P), (1, DC - P)):
                    t = mm(ps[0:KC, :], ctxT[2][0:n, k, b * KC:(b + 1) * KC], w3[0:n, k, :], k == 0, k == 1, [tw, pw])
                T["k1c", b] = yield from key_tail(ps, t, KC, b, S, TPB)
            p_ring.give(w, t)

        def keys1_job(tile):
            yield from until(("xt", 2, tile // CT))
            yield from until("h_done0")
            w = yield from until(("w", "a1"))
            t0 = tile * P
            ps, pw = yield from bank.get()
            for k in range(KD):
                t = mm3(ps[:, :], xt(k, t0, t0 + P), wv(w, 512 + k * 512, 512 + (k + 1) * 512), k == 0, k == KD - 1,
                        [T["xt", 2, tile // CT], w.ready, pw])
            out = yield from key_tail(ps, t, P, tile // TPB, (tile % TPB) * P, tile % TPB)
            T["k1", tile] = out

        def query1_job(tile):
            b = tile // TPB
            ticket, _ = yield from attention1_ring.get()
            w = yield from until(("w", "a1"))
            yield from until(("xt", 2, tile // CT))
            t0 = tile * P
            ps, pw = yield from bank.get()
            for k in range(KD):
                t = mm3(ps[:, 0:D], xt(k, t0, t0 + P), wv(w, k * D, (k + 1) * D), k == 0, k == KD - 1,
                        [T["xt", 2, tile // CT], w.ready, pw])
            T["xt_last", 2, tile // CT] = t
            qn, war = yield from pt_ring.get()
            tn, war2 = yield from tiny_ring.get()
            s = rms_scale(qn, ps[:, 0:D], 4, P, tn, t, [war, war2])
            s = DV.tt(qn[:, 0:D].rearrange("p (h d) -> p h d", d=64), ps[:, 0:D].rearrange("p (h d) -> p h d", d=64),
                      along(tn[:, 4:8], 2, 64), ALU.mult, [s])
            tiny_ring.give(tn, s)
            bank.give(ps, s)
            yield
            ps, pw = yield from bank.get()
            for e in range(2):
                t = transpose(ps[:, e * P:(e + 1) * P], qn[:, e * P:(e + 1) * P], [s, pw])
            qT = qn
            t = DV.ts(qT[:, 0:2 * P], ps[:, 0:2 * P], col("qng"), 0.125, ALU.mult, ALU.mult, [t])
            bank.give(ps, t)
            yield
            kc = yield from until(("k1c", b))
            ps, pw = yield from bank.get()
            for h in (0, 2, 1, 3):
                r = 64 * (h % 2)
                if h == 1:
                    PE.wait([ts_])
                ts_ = mm(ps[:, h * KC:(h + 1) * KC], qT[r:r + 64, (h // 2) * P:(h // 2 + 1) * P],
                         KT1[r:r + 64, h // 2, b, S:S + KC], True, True, [t, kc, pw])
            sc, war = yield from pt_ring.get()
            s3 = sc[:, 0:4 * KC].rearrange("p (h k) -> p h k", k=KC)
            a = DV.tt(s3, ps[:, 0:4 * KC].rearrange("p (h k) -> p h k", k=KC), along(maskf[:, b, :], 1, 4), ALU.mult,
                      [ts_, war, t_m])
            bank.give(ps, a)
            a = DV.tt(s3, s3, along(maskn[:, b, :], 1, 4), ALU.add, [a])
            ops = yield from bank.get()
            T["q1", tile] = [qT, t, sc, a, ops, ticket]

        def head1_job(tile, h):
            b = tile // TPB
            qT, tq, sc, tc, (ops, opw), _ = yield from until(("q1", tile))
            for j in range(TPB):
                yield from until(("k1", b * TPB + j))
            hticket, _ = yield from head_ring.get()
            r, e = 64 * (h % 2), h // 2
            tn, war2 = yield from tiny_ring.get()
            pb, war = yield from p_ring.get()
            pss = []
            for j in range(2):
                ps, pw = yield from bank.get()
                keys = [T["k1", b * TPB + 4 * j + i] for i in range(4)]
                t = mm(ps[:, :], qT[r:r + 64, e * P:(e + 1) * P], KT1[r:r + 64, e, b, j * 512:(j + 1) * 512], True, True,
                       [tq, pw, keys])
                m = DV.reduce(tn[:, j:j + 1], ps[:, :], ALU.max, [t, war2])
                pss.append((ps, t))
            m = DV.reduce(tn[:, 2:3], sc[:, h * KC:(h + 1) * KC], ALU.max, [tc])
            m = DV.reduce(tn[:, 3:4], tn[:, 0:3], ALU.max, [m], negate=True)
            for j, (ps, t) in enumerate(pss):
                a = AC.act(pb[:, j * 512:(j + 1) * 512], ps[:, :], ACT.Exp, [m, war], bias=tn[:, 3:4],
                           accum=tn[:, 4 + j:5 + j])
                bank.give(ps, a)
            a = AC.act(pb[:, S:S + KC], sc[:, h * KC:(h + 1) * KC], ACT.Exp, [m], bias=tn[:, 3:4], accum=tn[:, 6:7])
            yield
            s = DV.reduce(tn[:, 7:8], tn[:, 4:7], ALU.add, [a])
            s = DV.add(lambda e: e.reciprocal(tn[:, 8:9], tn[:, 7:8]), [s])
            a = DV.ts(pb[:, 0:S + KC], pb[:, 0:S + KC], tn[:, 8:9], None, ALU.mult, None, [s])
            tiny_ring.give(tn, a)
            yield
            for j in range(3):
                ps, pw = yield from bank.get()
                n = 4 if j < 2 else 1
                kp = P if j < 2 else KC
                for i in range(n):
                    c0 = j * 512 + i * P
                    t = transpose(ps[0:kp, i * P:(i + 1) * P], pb[:, c0:c0 + kp], [a, pw], signal=i == n - 1)
                pT, war = yield from pt_ring.get()
                if j == 1:
                    cp = DV.copy(pT[0:kp, 0:n * P], ps[0:kp, 0:n * P], [t, war])
                else:
                    cp = AC.act(pT[0:kp, 0:n * P], ps[0:kp, 0:n * P], ACT.Copy, [t, war])
                bank.give(ps, cp)
                yield
                if j == 0 and h > 1:
                    yield from until(("o1_open", tile, h - 2))
                for i in range(n):
                    blk = 4 * j + i
                    PE.wait([cp, opw, T["k1c", b]])
                    to = PE.add(lambda e_, o=ops[r:r + 64, e * P:(e + 1) * P], v=V1[0:kp, b, blk, h * 64:(h + 1) * 64],
                                p=pT[0:kp, i * P:(i + 1) * P], f=blk == 0 and h < 2, z=blk == TPB:
                                e_.matmul(o, v, p, start=f, stop=z, skip_group_check=True), signal=i == n - 1)
                T["o1_open", tile, h] = True
                pt_ring.give(pT, to)
            p_ring.give(pb, t)
            head_ring.give(hticket)
            T["o1", tile, h] = to
            yield

        def out1_job(tile):
            for h in range(4):
                yield from until(("o1", tile, h))
            qT, tq, sc, tc, (ops, opw), _ = T["q1", tile]
            w = T["w", "a1"]
            to = [T["o1", tile, h] for h in range(4)]
            pt_ring.give(qT, to)
            pt_ring.give(sc, to)
            ot, war = yield from ot_ring.get()
            ps, t = yield from project_out(ot, (ops, to), 2, w, 1536, war)
            ot_ring.give(ot, t)
            w.done(t)
            a = residual(tile, ps[:, 0:D], 1, t)
            bank.give(ps, a)
            T["x", tile] = a
            T["x_ready", 3, tile] = a
            attention1_ring.give(T["q1", tile][5])
            last_of("h_done1", TILES, t)
            yield

        def router_job(layer, key, c, idx):
            yield from until(("xt", key, c))
            gate = 4 + layer
            if c == 0:
                T["bdown", idx] = SY.dma(bdown[:, :], A["bdown"][idx], [T.get("bdown_read")], s_bdown)
            ps, pw = yield from bank.get()
            for i in range(CT):
                for k in range(KD):
                    t0 = (c * CT + i) * P
                    t = mm3(ps[:, i * 8:(i + 1) * 8], xt(k, t0, t0 + P), (gateh[:, idx, k, :], gatel[:, idx, k, :]),
                            k == 0, k == KD - 1, [T["xt", key, c], pw, t_gate])
            sm = small
            L = [sm[:, i, :].rearrange("p (t e) -> p t e", e=8) for i in range(8)]
            lf = [sm[:, i, :] for i in range(8)]
            a = DV.tt(L[0], ps[:, 0:32].rearrange("p (t e) -> p t e", e=8), along(gbias[:, idx, :], 1, CT), ALU.add,
                      [t, loaded, T.get("small")])
            bank.give(ps, a)
            nE = EXPERTS
            out = RW[:, c, :, 0:nE]
            if layer == 0:
                a = AC.act(lf[1], lf[0], ACT.Tanh, [a], scale=0.5)
                a = DV.ts(lf[1], lf[1], 0.5, 0.5, ALU.mult, ALU.add, [a])
            else:
                for i in range(CT):
                    m = DV.add(lambda e, i=i: e.max(L[2][:, i, :], L[0][:, i, :]), [a])
                a = DV.tt(L[3], L[0], along(L[2][:, :, 0], 2, nE), ALU.subtract, [m])
                a = AC.act(lf[1], lf[3], ACT.Exp, [a])
                if layer == 3:
                    q = DV.tt(L[3], L[0], along(L[2][:, :, 1], 2, nE), ALU.is_ge, [a])
                    a = DV.tt(L[1], L[1], L[3], ALU.mult, [q, a])
                s = DV.reduce(lf[4][:, 0:CT], L[1], ALU.add, [a])
                s = DV.add(lambda e: e.reciprocal(lf[4][:, 8:8 + CT], lf[4][:, 0:CT]), [s])
                a = DV.tt(L[1], L[1], along(lf[4][:, 8:8 + CT], 2, nE), ALU.mult, [s])
            if layer < 3:
                for i in range(CT):
                    m = DV.add(lambda e, i=i: e.max(L[2][:, i, :], L[1][:, i, :]), [a])
                for i in range(CT):
                    n = DV.add(lambda e, i=i: e.max_index(lf[5][:, i * 8:(i + 1) * 8].bitcast(U32), L[2][:, i, :],
                                                          L[1][:, i, :]), [m])
                n = DV.copy(lf[6], lf[5].bitcast(U32), [n])
                io = along(iota[:, 0:nE], 1, CT)
                q0 = DV.tt(L[3], io, along(L[6][:, :, 0], 2, nE), ALU.is_equal, [n])
                q1 = DV.tt(L[5], io, along(L[6][:, :, 1], 2, nE), ALU.is_equal, [n])
                q = DV.tt(L[3], L[3], L[5], ALU.add, [q0, q1])
                a = DV.tt(L[1], L[1], L[3], ALU.mult, [q])
            if layer == 0:
                s = DV.tt(lf[4][:, 0:CT], L[2][:, :, 0], L[2][:, :, 1], ALU.add, [m, a])
                s = DV.ts(lf[4][:, 0:CT], lf[4][:, 0:CT], 1e-6, None, ALU.add, None, [s])
                s = DV.add(lambda e: e.reciprocal(lf[4][:, 8:8 + CT], lf[4][:, 0:CT]), [s])
                a = DV.tt(L[1], L[1], along(lf[4][:, 8:8 + CT], 2, nE), ALU.mult, [s])
                s = DV.memset(RW[:, c, :, nE:nE + 1], 0.1, [T.get(("rw_free", c))])
                s = DV.ts(RW[:, c, :, nE:nE + 1], RW[:, c, :, nE:nE + 1], tg[:, gate:gate + 1], None, ALU.mult, None, [s])
            a = DV.ts(out, L[1], tg[:, gate:gate + 1], None, ALU.mult, None, [a, T.get(("rw_free", c))])
            T["small"] = a
            T["rw", key, c] = a
            yield
            ne = nE + 1 if layer == 0 else nE
            ps, pw = yield from bank.get()
            for i in range(CT):
                t = transpose(ps[0:ne, i * P:(i + 1) * P], RW[:, c, i, 0:ne], [a, pw], signal=i == CT - 1)
            RWT, war = yield from pt_ring.get()
            cp = AC.act(RWT[0:ne, :], ps[0:ne, :], ACT.Copy, [t, war])
            bank.give(ps, cp)
            yield
            for i in range(CT):
                ps, pw = yield from bank.get()
                t = mm(ps[:, 0:D], RWT[0:ne, i * P:(i + 1) * P], bdown[0:ne, :], True, True, [cp, pw, T["bdown", idx]])
                tile = c * CT + i
                a = DV.tt(Xs[:, tile, :], Xs[:, tile, :], ps[:, 0:D], ALU.add,
                          [t, T["x", tile], T["x_read", key, tile]])
                T["x", tile] = a
                bank.give(ps, a)
            pt_ring.give(RWT, t)
            T["bdown_read"] = t
            T["routed", key, c] = a
            yield

        def expert_job(layer, key, item, c, nitems):
            e = item // 2
            yield from until(("routed", key, c))
            w = yield from until(("w", f"f{layer}_{item}"))
            (hh, hl), hwar = yield from h_ring.get()
            if layer > 1:
                hwar = [hwar, T["h_done1"]]
            t0 = c * CTOK
            bias = "bu0" if layer == 0 else "b13"
            ready = []
            for f in range(4):
                ps, pw = yield from bank.get()
                for k in range(KD):
                    a0 = k * HALF + f * P
                    t = mm3(ps[:, :], wv(w, a0, a0 + P), xt(k, t0, t0 + CTOK), k == 0, k == KD - 1,
                            [T["xt", key, c], w.ready, pw])
                g, gwar = yield from g_ring.get()
                a = AC.act(g[:, :], ps[:, :], ACT.Gelu, [t, gwar, hwar if layer > 1 else None],
                           bias=col(bias, item * 4 + f))
                bank.give(ps, a)
                ready.append(split(g[:, :], hh[:, f * CTOK:(f + 1) * CTOK], hl[:, f * CTOK:(f + 1) * CTOK], a, hwar))
                g_ring.give(g, *ready[-1])
            T["xt_last", key, c] = t
            yield
            yield
            for i in range(CT):
                ps, pw = yield from bank.get()
                for f in range(4):
                    h0 = f * CTOK + i * P
                    t = mm3(ps[:, 0:D], (hh[:, h0:h0 + P], hl[:, h0:h0 + P]), wv(w, 1024 + f * D, 1024 + (f + 1) * D),
                            f == 0, f == 3, [ready[f], pw])
                tile = c * CT + i
                a = DV.stt(Xs[:, tile, :], ps[:, 0:D], RW[:, c, i, e:e + 1], Xs[:, tile, :], ALU.mult, ALU.add,
                           [t, T["x", tile], T["rw", key, c]])
                bank.give(ps, a)
                T["x", tile] = a
                if item == nitems - 1:
                    T["x_ready", key + 1, tile] = a
            T["rw_free", c] = a
            h_ring.give((hh, hl), t)
            w.done(t)
            if item == nitems - 1:
                last_of(f"h_done{layer}", CHUNKS, t)
            yield

        def linear_expert_job(key, item, c):
            yield from until(("routed", key, c))
            w = yield from until(("w", f"f1_{item}"))
            for i in range(CT):
                tile = c * CT + i
                t0 = tile * P
                for j in range(2):
                    ps, pw = yield from bank.get()
                    for k in range(KD):
                        a0 = k * 1024 + j * 512
                        t = mm3(ps[:, :], xt(k, t0, t0 + P), wv(w, a0, a0 + 512), k == 0, k == KD - 1,
                                [T["xt", key, c], w.ready, pw])
                    for q in range(2):
                        e = item * 4 + j * 2 + q
                        a = DV.stt(Xs[:, tile, :], ps[:, q * D:(q + 1) * D], RW[:, c, i, e:e + 1], Xs[:, tile, :],
                                   ALU.mult, ALU.add, [t, T["x", tile], T["rw", key, c]])
                        T["x", tile] = a
                    bank.give(ps, a)
                if item == 1:
                    T["x_ready", key + 1, tile] = a
            T["xt_last", key, c] = t
            T["rw_free", c] = a
            w.done(t)
            yield

        def mlp_job(key, item, c):
            yield from until(("xt", key, c))
            w = yield from until(("w", f"m2_{item}"))
            (hh, hl), hwar = yield from h_ring.get()
            hwar = [hwar, (yield from until("h_done1"))]
            t0 = c * CTOK
            ready = []
            for f in range(2):
                tiles = []
                for part in range(2):
                    ps, pw = yield from bank.get()
                    for k in range(KD):
                        a0 = part * 512 + k * D + f * P
                        t = mm3(ps[:, :], wv(w, a0, a0 + P), xt(k, t0, t0 + CTOK), k == 0, k == KD - 1,
                                [T["xt", key, c], w.ready, pw])
                    tiles.append((ps, t))
                g, gwar = yield from g_ring.get()
                (pg, tg_), (pu, tu) = tiles
                a = AC.act(g[:, :], pg[:, :], ACT.Silu, [tg_, gwar, hwar], bias=col("bg2", item * 2 + f))
                bank.give(pg, a)
                a = DV.stt(g[:, :], pu[:, :], col("bu2", item * 2 + f), g[:, :], ALU.add, ALU.mult, [a, tu])
                bank.give(pu, a)
                ready.append(split(g[:, :], hh[:, f * CTOK:(f + 1) * CTOK], hl[:, f * CTOK:(f + 1) * CTOK], a, hwar))
                g_ring.give(g, *ready[-1])
            yield
            yield
            for i in range(CT):
                ps, pw = yield from bank.get()
                for f in range(2):
                    h0 = f * CTOK + i * P
                    t = mm3(ps[:, 0:D], (hh[:, h0:h0 + P], hl[:, h0:h0 + P]), wv(w, 1024 + f * D, 1024 + (f + 1) * D),
                            f == 0, f == 1, [ready[f], pw])
                tile = c * CT + i
                if item == 0:
                    b = PL.tt(Xs[:, tile, :], Xs[:, tile, :], row("bd2"), ALU.add,
                              [T["x", tile], T["x_read", key, tile], t_rows])
                    T["x", tile] = b
                a = DV.stt(Xs[:, tile, :], ps[:, 0:D], tg[:, 6:7], Xs[:, tile, :], ALU.mult, ALU.add,
                           [t, T["x", tile], T["x_read", key, tile]])
                bank.give(ps, a)
                T["x", tile] = a
                T["mlp", item, tile] = a
            h_ring.give((hh, hl), t)
            w.done(t)
            yield

        def peer_job(key, tile):
            c = tile // CT
            yield from until(("xt", key, c))
            wq = yield from until(("w", "pq"))
            keys_ready = T["keys"]
            kv2_done = yield from until("kv2_done")
            t0 = tile * P
            ps, pw = yield from bank.get()
            for k in range(KD):
                t = mm3(ps[:, :], xt(k, t0, t0 + P), wv(wq, k * 512, (k + 1) * 512), k == 0, k == KD - 1,
                        [T["xt", key, c], wq.ready, pw])
            wq.done(t)
            qs, war = yield from pt_ring.get()
            a = AC.act(qs[:, :], ps[:, :], ACT.Copy, [t, war])
            bank.give(ps, a)
            yield
            ps, pw = yield from bank.get()
            for j in range(4):
                t = transpose(ps[:, j * P:(j + 1) * P], qs[:, j * P:(j + 1) * P], [a, pw], signal=j == 3)
            pt_ring.give(qs, t)
            qT, war = yield from pt_ring.get()
            a = AC.act(qT[:, :], ps[:, :], ACT.Copy, [t, war])
            bank.give(ps, a)
            yield
            ps, pw = yield from bank.get()
            for j in range(4):
                t = mm(ps[:, j * P:(j + 1) * P], qT[:, j * P:(j + 1) * P], KEYS[:, j, :], True, True,
                       [a, pw, keys_ready], signal=j == 3)
            pt_ring.give(qT, t)
            scratch, _ = yield from scratch_ring.get()
            sim, war = yield from sim_ring.get()
            t = AC.act(sim[:, :, :].rearrange("p a k -> p (a k)"), ps[:, :], ACT.Copy, [t, war])
            bank.give(ps, t)
            yield
            for j in range(8):
                m = DV.add(lambda e, j=j: e.max(V8[:, j, :], sim[:, j, :]), [t, war])
            for j in range(8):
                n = DV.add(lambda e, j=j: e.max_index(I8[:, j, :], V8[:, j, :], sim[:, j, :]), [m])
            n = DV.copy(I8f[:, :, :], I8[:, :, :], [n])
            g4 = GRID[:, 0, :].rearrange("p (h a b) -> p h a b", a=8, b=8)
            gh = [GRID[:, i, :].rearrange("p (h c) -> p h c", h=4) for i in range(2)]
            for h in range(4):
                a = DV.tt(g4[:, h, :, :], along(V8[:, h, :], 2, 8), along(V8[:, 4 + h, :], 1, 8), ALU.add, [m])
            for h in range(4):
                m8 = DV.add(lambda e, h=h: e.max(T8[:, h, :], gh[0][:, h, :]), [a])
            for h in range(4):
                r = DV.add(lambda e, h=h: e.match_replace(gh[1][:, h, :], T8[:, h, :], gh[0][:, h, :], -FLT_MAX), [m8])
            sel = GRID[:, 1, :]
            r = DV.tt(sel, sel, GRID[:, 0, :], ALU.not_equal, [r])
            ca = DV.reduce(CA[:, :, :].rearrange("p h a -> p (h a)"), sel.rearrange("p (h b) -> p h b", b=8), ALU.add, [r])
            yield
            q = DV.tt(EXB[:, 0:64].rearrange("p (h k) -> p h k", h=4), sim[:, 0:4, 0:16], along(V8[:, 0:4, 0], 2, 16),
                      ALU.subtract, [m])
            q = DV.tt(EXB[:, 64:320].rearrange("p (h k) -> p h k", h=4), sim[:, 4:8, :], along(V8[:, 4:8, 0], 2, 64),
                      ALU.subtract, [m])
            q = DV.tt(EXB[:, 320:352].rearrange("p (h k) -> p h k", h=4), T8[:, :, :], along(T8[:, :, 0], 2, 8),
                      ALU.subtract, [m8])
            sim_ring.give(sim, q, n)
            q2 = DV.tt(gh[0], gh[0], along(T8[:, :, 0], 2, 64), ALU.subtract, [r])
            q = AC.act(EXB[:, :], EXB[:, :], ACT.Exp, [q])
            q2 = AC.act(GRID[:, 0, :], GRID[:, 0, :], ACT.Exp, [q2])
            z = DV.reduce(pz[:, 0:4], EXB[:, 320:352].rearrange("p (h k) -> p h k", h=4), ALU.add, [q])
            z = DV.add(lambda e: e.reciprocal(pz[:, 4:8], pz[:, 0:4]), [z])
            ex = EXB[:, 0:64].rearrange("p (h k) -> p h k", h=4)
            ey = EXB[:, 64:320].rearrange("p (h k) -> p h k", h=4)
            ez = DV.tt(ex, ex, along(pz[:, 4:8], 2, 16), ALU.mult, [z])
            g_ = DV.tt(GRID[:, 0, :], GRID[:, 0, :], sel, ALU.mult, [q2, r])
            cl = DV.reduce(T8[:, :, :].rearrange("p h a -> p (h a)"), GRID[:, 0, :].rearrange("p (h b) -> p h b", b=8),
                           ALU.add, [g_, q])
            cl = DV.stt(T8[:, :, :].rearrange("p h a -> p (h a)"), I8f[:, 0:4, :].rearrange("p h a -> p (h a)"), 16.0,
                        T8[:, :, :].rearrange("p h a -> p (h a)"), ALU.is_ge, ALU.mult, [cl, n])
            cl = DV.tt(T8[:, :, :], T8[:, :, :], along(pz[:, 4:8], 2, 8), ALU.mult, [cl, z])
            cl = DV.reduce(pz[:, 8:9], T8[:, :, :].rearrange("p h a -> p (h a)"), ALU.add, [cl])
            yield
            oh = SCR[:, 0:512].rearrange("p (h x a) -> p h x a", h=4, x=16)
            war = [T.get("scr"), kv2_done]
            for h in range(4):
                u = DV.tt(oh[:, h], along(iota[:, 0:16], 2, 8), along(I8f[:, h, :], 1, 16), ALU.is_equal, [n, war])
            for h in range(4):
                v = DV.tt(oh[:, h], oh[:, h], along(CA[:, h, :], 1, 16), ALU.mult, [u, ca])
            v = DV.reduce(CX[:, :, :].rearrange("p h x -> p (h x)"), SCR[:, 0:512].rearrange("p (h a) -> p h a", a=8),
                          ALU.add, [v])
            cx = DV.ts(CX[:, :, :], CX[:, :, :], -100.0, None, ALU.add, None, [v])
            oy = SCR[:, :].rearrange("p (h y b) -> p h y b", h=4, y=64)
            for h in range(4):
                u = DV.tt(oy[:, h], along(iota[:, 0:64], 2, 8), along(I8f[:, 4 + h, :], 1, 64), ALU.is_equal, [cx, war])
            u = DV.tt(SCR[:, :].rearrange("p (c b) -> p c b", b=8), SCR[:, :].rearrange("p (c b) -> p c b", b=8),
                      along(rank8[:, :], 1, 256), ALU.mult, [u])
            ry = DV.reduce(RY[:, :, :].rearrange("p h y -> p (h y)"), SCR[:, :].rearrange("p (c b) -> p c b", b=8),
                           ALU.add, [u])
            yield
            Sd, war = yield from p_ring.get()
            s3 = Sd[:, 0:1024].rearrange("p (x y) -> p x y", y=64)
            A3 = SCR[:, 0:1024].rearrange("p (x y) -> p x y", y=64)
            B3 = SCR[:, 1024:2048].rearrange("p (x y) -> p x y", y=64)
            hs, hwar2 = yield from p_ring.get()
            last, pb = ry, None
            for h in range(4):
                pb = PL.tt(B3, along(ex[:, h, :], 2, 64), along(ey[:, h, :], 1, 16), ALU.mult, [ez, last, pb, T.get("scr")])
                ma = DV.tt(A3, along(CX[:, h, :], 2, 64), along(RY[:, h, :], 1, 16), ALU.is_gt, [ry, last])
                if h == 0:
                    last = DV.tt(s3, A3, B3, ALU.mult, [ma, pb, war])
                else:
                    last = DV.tt(A3, A3, B3, ALU.mult, [ma, pb])
                    last = DV.tt(s3, s3, A3, ALU.add, [last])
            T["scr"] = [last, pb]
            last = DV.tt(Sd[:, 1023:1024], Sd[:, 1023:1024], pz[:, 8:9], ALU.add, [last, cl])
            scratch_ring.give(scratch)
            yield
            wd = yield from until(("w", "pd"))
            for j in range(2):
                ps, pw = yield from bank.get()
                for k in range(KD):
                    a0 = k * 1024 + j * 512
                    t = mm3(ps[:, :], xt(k, t0, t0 + P), wv(wd, a0, a0 + 512), k == 0, k == KD - 1, [wd.ready, pw])
                a = AC.act(hs[:, j * 512:(j + 1) * 512], ps[:, :], ACT.Silu, [t, hwar2])
                bank.give(ps, a)
            wd.done(t)
            T["xt_last", key, c] = t
            a = DV.tt(Sd[:, 0:1024], Sd[:, 0:1024], hs[:, 0:1024], ALU.mult, [a, last])
            p_ring.give(hs, a)
            yield
            wu = yield from until(("w", "pu"))
            (hh, hl), hwar = yield from h_ring.get()
            ready = []
            for j in range(2):
                ps, pw = yield from bank.get()
                for i in range(4):
                    t = transpose(ps[:, i * P:(i + 1) * P], Sd[:, (4 * j + i) * P:(4 * j + i + 1) * P], [a, pw],
                                  signal=i == 3)
                b1 = AC.act(hh[:, j * 512:(j + 1) * 512], ps[:, :], ACT.Copy, [t, hwar, T["h_done1"]])
                b2 = DV.tt(hl[:, j * 512:(j + 1) * 512], ps[:, :], hh[:, j * 512:(j + 1) * 512].bitcast(F32),
                           ALU.subtract, [b1, hwar])
                bank.give(ps, b2)
                ready.append([b1, b2])
            p_ring.give(Sd, t)
            yield
            ps, pw = yield from bank.get()
            for i in range(8):
                t = mm3(ps[:, 0:D], (hh[:, i * P:(i + 1) * P], hl[:, i * P:(i + 1) * P]), wv(wu, i * D, (i + 1) * D),
                        i == 0, i == 7, [ready[i // 4], pw, wu.ready])
            wu.done(t)
            h_ring.give((hh, hl), t)
            for i in range(MLP_PARTS):
                yield from until(("mlp", i, tile))
            a = DV.stt(Xs[:, tile, :], ps[:, 0:D], tg[:, 6:7], Xs[:, tile, :], ALU.mult, ALU.add, [t, T["x", tile]])
            bank.give(ps, a)
            T["x", tile] = a
            T["x_ready", key + 1, tile] = a
            yield

        def keys_job():
            yield from until("h_done0")
            T["keys"] = SY.dma(KEYS[:, :, :].rearrange("p j k -> p (j k)"), A["keys"], [T["h_done0"]], s_keys)

        def epoch_job(name):
            for q, n in ((PE, "pe"), (AC, "act"), (DV, "dve"), (PL, "pool")):
                q.epoch(sem(f"{n}_{name}"))
            return
            yield

        jobs = [ctx_job(), ctx0_job()]
        for i in range(TILES):
            T["x_ready", 0, i] = T["x", i]

        def attention_phase(layer, gain=None, second=False, ahead=1):
            for c in range(CHUNKS + ahead):
                if c < CHUNKS:
                    jobs.append(tokens_job(2 * layer, c, gain, second))
                if c >= ahead:
                    jobs.extend(attention_job(layer, t) for t in range((c - ahead) * CT, (c - ahead + 1) * CT))

        def expert_phase(layer, nitems):
            for c in range(CHUNKS):
                jobs.append(tokens_job(2 * layer + 1, c))
                jobs.append(router_job(layer, 2 * layer + 1, c, {0: 0, 1: 1, 3: 2}[layer]))
            for item in range(nitems):
                for c in range(CHUNKS):
                    jobs.append(expert_job(layer, 2 * layer + 1, item, c, nitems) if layer != 1
                                else linear_expert_job(3, item, c))

        attention_phase(0, ("ln1g", "ln1b"), True)
        jobs.append(epoch_job("experts0"))
        jobs += [ctx2_job(), ctx3_job()]
        expert_phase(0, L0_HALVES)
        jobs.append(epoch_job("attention1"))
        jobs.append(keys_job())
        jobs.append(keys1_ctx_job())
        for c in range(CHUNKS):
            jobs.append(tokens_job(2, c, ("llg", "llb"), True))
            jobs.extend(keys1_job(t) for t in range(c * CT, (c + 1) * CT))
        for t in range(TILES):
            jobs.append(query1_job(t))
            jobs.extend(head1_job(t, h) for h in range(4))
            jobs.append(out1_job(t))
        jobs.append(epoch_job("experts1"))
        expert_phase(1, 2)
        jobs.append(epoch_job("attention2"))
        attention_phase(2)
        jobs.append(epoch_job("experts2"))
        for c in range(CHUNKS):
            jobs.append(tokens_job(5, c))
        for item in range(MLP_PARTS):
            for c in range(CHUNKS):
                jobs.append(mlp_job(5, item, c))
        jobs.extend(peer_job(5, t) for t in range(TILES))
        jobs.append(epoch_job("attention3"))
        attention_phase(3)
        jobs.append(epoch_job("experts3"))
        expert_phase(3, L3_HALVES)
        interleave(jobs, weights_job(), 8, (PE, AC, DV, PL, SY))

        out_v = A["out"].rearrange("b (n p) d -> p (b n) d", p=P)
        for c in range(CHUNKS):
            SY.dma(out_v[:, c * CT:(c + 1) * CT, :], Xs[:, c * CT:(c + 1) * CT, :],
                   [T["x", i] for i in range(c * CT, (c + 1) * CT)], s_out)
        SY.wait([tuple(s_out)])
        block = ctx.enter_context(nc.Block())
        block.sync(SY.replay)
        block.tensor(PE.replay)
        block.scalar(AC.replay)
        block.vector(DV.replay)
        block.gpsimd(PL.replay)


def lay_out(np, inputs):
    def kmajor(w):
        k, n = w.shape
        return np.ascontiguousarray(w.reshape(k // P, P, n).transpose(1, 0, 2).reshape(P, -1))

    def block(*parts):
        out = np.zeros((P, WB), np.float32)
        at = 0
        for p in parts:
            out[:, at:at + p.shape[1]] = p
            at += p.shape[1]
        return out

    g = inputs
    blocks = [block(kmajor(g["L0_xattn_Wq"]), kmajor(g["L0_xattn_Wo"]))]
    for e in range(EXPERTS + 1):
        up = g["L0_ffn_Wu"][e] if e < EXPERTS else g["L0_ffn_sWu"]
        down = g["L0_ffn_Wd"][e] if e < EXPERTS else g["L0_ffn_sWd"]
        for i in range(2):
            blocks.append(block(kmajor(up[i * HALF:(i + 1) * HALF].T), kmajor(down[:, i * HALF:(i + 1) * HALF].T)))
    blocks.append(block(kmajor(g["L1_xattn_Wq"].T), kmajor(g["L1_xattn_Wlkv"].T), kmajor(g["L1_xattn_Wo"].T)))
    for i in range(2):
        w = g["L1_ffn_expert_w"][4 * i:4 * i + 4]
        blocks.append(block(kmajor(w.transpose(2, 0, 1).reshape(D, 4 * D))))
    blocks.append(block(kmajor(g["L2_xattn_Wq"]), kmajor(g["L2_xattn_Wo"])))
    for i in range(MLP_PARTS):
        s = slice(i * 256, (i + 1) * 256)
        blocks.append(block(kmajor(g["L2_ffn_Wg"][:, s]), kmajor(g["L2_ffn_Wu"][:, s]), kmajor(g["L2_ffn_Wd"][s])))
    blocks.append(block(kmajor(g["L2_ffn_Wq"])))
    blocks.append(block(kmajor(g["L2_ffn_down_embed"].T)))
    blocks.append(block(kmajor(g["L2_ffn_up_embed"])))
    blocks.append(block(kmajor(g["L3_xattn_Wq"]), kmajor(g["L3_xattn_Wo"])))
    for e in range(EXPERTS):
        for i in range(2):
            s = slice(i * HALF, (i + 1) * HALF)
            blocks.append(block(kmajor(g["L3_ffn_W1"][e][:, s]), kmajor(g["L3_ffn_W2"][e][s])))
    blocks = np.stack(blocks)

    cols = np.zeros((P, NCOLS), np.float32)

    def put(name, v):
        v = np.asarray(v, np.float32).reshape(-1)
        at, n = COLS[name]
        full = np.zeros(n * P, np.float32)
        full[:v.size] = v
        cols[:, at:at + n] = full.reshape(n, P).T
    put("ln1g", g["L0_xattn_ln1_g"]); put("ln1b", g["L0_xattn_ln1_b"])
    put("ln2g", g["L0_xattn_ln2_g"]); put("ln2b", g["L0_xattn_ln2_b"])
    put("bq0", g["L0_xattn_bq"]); put("bk0", g["L0_xattn_bk"])
    put("bu0", np.concatenate([g["L0_ffn_bu"].reshape(-1), g["L0_ffn_sbu"]]))
    put("lxg", g["L1_xattn_ln_x_g"]); put("lxb", g["L1_xattn_ln_x_b"])
    put("llg", g["L1_xattn_ln_l_g"]); put("llb", g["L1_xattn_ln_l_b"])
    put("qng", np.concatenate([g["L1_xattn_qn_g"]] * 2)); put("kng", np.concatenate([g["L1_xattn_kn_g"]] * 2))
    put("bg2", g["L2_ffn_bg"]); put("bu2", g["L2_ffn_bu"]); put("b13", g["L3_ffn_b1"])
    p = np.arange(P)
    cols[:, COLS["hm4"][0]:COLS["hm4"][0] + 4] = (p[:, None] % 64 // 16 == np.arange(4)[None])
    cols[:, COLS["hm2"][0]:COLS["hm2"][0] + 2] = (p[:, None] // 64 == np.arange(2)[None])

    bdown = np.zeros((3, EXPERTS + 1, D), np.float32)
    bdown[0] = np.concatenate([g["L0_ffn_bd"], g["L0_ffn_sbd"][None]])
    bdown[1, :EXPERTS] = g["L1_ffn_expert_b"]
    bdown[2, :EXPERTS] = g["L3_ffn_b2"]
    keys = np.zeros((P, 4, P), np.float32)
    for half in range(2):
        for h in range(4):
            r = 64 * (h % 2)
            keys[r:r + 64, half * 2 + h // 2, r:r + 64] = g["L2_ffn_keys"][h, :, half, :].T
    return {
        "x": g["x"], "ctx": g["ctx_768"], "mask": np.ascontiguousarray(g["mask_BxS2_bk0"]).reshape(-1),
        "g": np.concatenate([g["g_xattn"], g["g_ffn"]]),
        "blocks": blocks, "cols": cols, "bdown": bdown, "keys": keys.reshape(P, -1),
        "ident": np.eye(P, dtype=np.float32),
        "iota": np.tile(np.arange(64, dtype=np.float32), (P, 1)),
        "rank8": np.tile(np.arange(8, dtype=np.float32) - 100, (P, 1)),
        "gates": np.concatenate([kmajor(g["L0_ffn_gate_w"].T), kmajor(g["L1_ffn_gate_w"].T), kmajor(g["L3_ffn_Wr"])], 1),
        "gbias": np.concatenate([g["L0_ffn_gate_bias"], g["L1_ffn_gate_b"], g["L3_ffn_br"]]),
        "rows": np.concatenate([g["L0_xattn_bo"], g["L1_xattn_bo"], g["L2_ffn_bd"], g["L3_xattn_bo"],
                                g["L2_xattn_ln_gamma"], g["L2_xattn_ln_beta"], g["L2_xattn_bq"], g["L2_xattn_bo"]]),
        "ctxrows": np.stack([g["L0_xattn_bv"], g["L2_xattn_bk"], g["L2_xattn_bv"]]),
        "ctxw0": np.concatenate([g["L0_xattn_Wk"], g["L0_xattn_Wv"]], 1),
        "ctxw1": g["L1_xattn_Wkv"].T,
        "ctxw2": np.concatenate([g["L2_xattn_Wk"], g["L2_xattn_Wv"]], 1),
        "ctxw3k": g["L3_xattn_Wk"], "ctxw3v": g["L3_xattn_Wv"],
    }


def kernel(**inputs):
    import numpy as np
    import concourse.bacc as bacc
    from concourse.bass_utils import run_bass_kernel_spmd

    laid = lay_out(np, {k: np.asarray(v) for k, v in inputs.items()})
    nc = bacc.Bacc("TRN2", target_bir_lowering=False, num_devices=1)
    arrays, A = {}, {}
    for name, a in laid.items():
        a = np.ascontiguousarray(a)
        arrays["in_" + name] = a
        A[name] = nc.dram_tensor("in_" + name, a.shape, mybir.dt.from_np(a.dtype), kind="ExternalInput").ap()
    A["out"] = nc.dram_tensor("out_0", (B, S, D), F32, kind="ExternalOutput").ap()
    build_program(nc, A)
    r = run_bass_kernel_spmd(nc, [arrays], core_ids=[0])
    return r.results[0]["out_0"]
```
